# Optimizing a Trainium2 kernel written in Bass

```python
import numpy as np
import jax
import jax.numpy as jnp

def _softmax(x, axis=-1):
    return jax.nn.softmax(x, axis=axis)

def _gelu(x):
    return jax.nn.gelu(x, approximate=True)

def _silu(x):
    return jax.nn.silu(x)

def _sigmoid(x):
    return jax.nn.sigmoid(x)

def _layernorm(x, axis=-1, eps=1e-05):
    m = jnp.mean(x, axis=axis, keepdims=True)
    v = jnp.var(x, axis=axis, keepdims=True)
    return (x - m) / jnp.sqrt(v + eps)

def _scatter_add(tgt, idx, src, axis=0):
    return tgt.at[idx].add(src)

def _segment_sum(src, seg, n):
    return jax.ops.segment_sum(src, seg, n)
kernel_name = 'mk_adj_preln_d2_adj_r2_df3a81'

def setup_inputs(seed: int=0):
    np.random.seed(seed)
    _w = jnp.asarray

    def _rec_inputs():
        import jax
        import jax.numpy as jnp
        _gk = jax.random.key(seed)
        x = 7.22e-05 + 1 * jax.random.normal(jax.random.fold_in(_gk, 1), (128, 128, 256), jnp.float32)
        _w = (1.0 + jnp.arange(128, dtype=jnp.float32)) ** (-0.5)
        _w = _w / _w.mean()
        _pij = jnp.clip(0.0625 * _w[:, None] * _w[None, :], 0.0, 1.0)
        _a = jax.random.uniform(jax.random.fold_in(_gk, 2), (128, 128, 128)) < _pij
        _af = _a.astype(jnp.float32)
        adj = _af
        return (x, adj)
    x, adj = _rec_inputs()

    def _L0_gnn_setup():
        import jax, jax.numpy as jnp
        import numpy as np
        IN_DIM = 256
        ATT_DIM = 64
        B, N = (4, 2048)
        key = jax.random.key(seed)
        k1, k2, k3, k4 = jax.random.split(key, 4)
        x = jax.random.normal(k1, (B, N, IN_DIM), dtype=jnp.float32)
        adj_matrix = (jax.random.uniform(k2, (B, N, N)) < 0.05).astype(jnp.float32)
        W_qk = jax.random.normal(k3, (2 * ATT_DIM, IN_DIM), dtype=jnp.float32) / np.sqrt(IN_DIM)
        W_v = jax.random.normal(k4, (IN_DIM, IN_DIM), dtype=jnp.float32) / np.sqrt(IN_DIM)
        return {'x': x, 'adj_matrix': adj_matrix, 'W_qk': W_qk, 'W_v': W_v}
    _L0_gnn_all = _L0_gnn_setup()
    _L0_gnn_in = {k: v for k, v in _L0_gnn_all.items() if k in ('W_qk', 'W_v')}
    del _L0_gnn_all

    def _L1_gnn_setup():
        import jax, jax.numpy as jnp
        import numpy as np
        B, N, DIN, DOUT, K = (4, 1024, 256, 256, 3)
        key = jax.random.key(seed)
        ks = jax.random.split(key, 8)
        X = jax.random.normal(ks[0], (B, N, DIN), dtype=jnp.float32)
        A = jax.random.uniform(ks[1], (B, N, N), dtype=jnp.float32)
        Wv = jax.random.normal(ks[2], (DIN, DOUT), dtype=jnp.float32) * 0.02
        bv = jax.random.normal(ks[3], (DOUT,), dtype=jnp.float32) * 0.02
        aw = jax.random.normal(ks[4], (2 * DOUT, 1), dtype=jnp.float32) * 0.05
        ab = jax.random.normal(ks[5], (1,), dtype=jnp.float32) * 0.05
        Wk = jax.random.normal(ks[6], (K, DIN, DOUT), dtype=jnp.float32) * 0.02
        bk = jax.random.normal(ks[7], (K, DOUT), dtype=jnp.float32) * 0.02
        return {'X': X, 'A': A, 'Wv': Wv, 'bv': bv, 'aw': aw, 'ab': ab, 'Wk': Wk, 'bk': bk}
    _L1_gnn_all = _L1_gnn_setup()
    _L1_gnn_in = {k: v for k, v in _L1_gnn_all.items() if k in ('Wv', 'bv', 'aw', 'ab', 'Wk', 'bk')}
    del _L1_gnn_all
    return {'x': x, 'adj': adj, 'L0_gnn_W_qk': _L0_gnn_in['W_qk'], 'L0_gnn_W_v': _L0_gnn_in['W_v'], 'L1_gnn_Wv': _L1_gnn_in['Wv'], 'L1_gnn_bv': _L1_gnn_in['bv'], 'L1_gnn_aw': _L1_gnn_in['aw'], 'L1_gnn_ab': _L1_gnn_in['ab'], 'L1_gnn_Wk': _L1_gnn_in['Wk'], 'L1_gnn_bk': _L1_gnn_in['bk']}

def reference(x, adj, L0_gnn_W_qk, L0_gnn_W_v, L1_gnn_Wv, L1_gnn_bv, L1_gnn_aw, L1_gnn_ab, L1_gnn_Wk, L1_gnn_bk):
    import jax
    import jax.numpy as jnp

    def _L0_gnn_ref(x, adj_matrix, W_qk, W_v):
        import jax, jax.numpy as jnp
        import numpy as np
        IN_DIM = 256
        ATT_DIM = 64
        B, N = (4, 2048)
        qk = jnp.einsum('bnd,ed->bne', x, W_qk)
        q, k = jnp.split(qk, 2, axis=-1)
        v = jnp.einsum('bnd,ed->bne', x, W_v)
        inv_scale = 1.0 / ATT_DIM ** 0.5
        scores = jnp.einsum('bnd,bmd->bnm', q, k) * inv_scale
        w = jnp.sum(scores * adj_matrix, axis=-1, keepdims=True)
        w = jax.nn.softmax(w, axis=1)
        return w * v

    def _L1_gnn_ref(X, A, Wv, bv, aw, ab, Wk, bk):
        import jax, jax.numpy as jnp
        import numpy as np
        B, N, DIN, DOUT, K = (4, 1024, 256, 256, 3)
        d = Wv.shape[1]
        Xw = X @ Wv + bv
        sj = Xw @ aw[:d, 0]
        si = Xw @ aw[d:, 0]
        e = jax.nn.leaky_relu(sj[:, None, :] + si[:, :, None] + ab[0], negative_slope=0.2)
        alpha_matrix = A * jnp.exp(e)
        transition = alpha_matrix / (jnp.sum(alpha_matrix, axis=-1, keepdims=True) + 1e-12)
        H = jnp.zeros(X.shape[:-1] + (d,), dtype=X.dtype)
        Xk = X
        for k in range(Wk.shape[0]):
            H = H + Xk @ Wk[k] + bk[k]
            Xk = jnp.einsum('bij,bjd->bid', transition, Xk)
        return jax.nn.relu(H)
    h = jnp.maximum(_layernorm(x, axis=-1), 0.0)
    x = x + _L0_gnn_ref(h, adj, L0_gnn_W_qk, L0_gnn_W_v)
    h = jnp.maximum(_layernorm(x, axis=-1), 0.0)
    x = x + _L1_gnn_ref(h, adj, L1_gnn_Wv, L1_gnn_bv, L1_gnn_aw, L1_gnn_ab, L1_gnn_Wk, L1_gnn_bk)
    return x

_drawn_inputs = setup_inputs


def setup_inputs(seed=0):
    import zlib

    import numpy as np

    out = dict(_drawn_inputs(seed))
    spreads = {}
    factors = {'L1_gnn_Wv': 8.0, 'L1_gnn_bv': 29.292, 'L1_gnn_aw': 8.0}
    for name, (base, spread) in spreads.items():
        noise = np.random.default_rng([zlib.crc32(name.encode()), seed]).standard_normal(out[name].shape)
        drawn = base * np.exp(spread * noise) if base else spread * noise
        out[name] = jnp.asarray(drawn.astype(out[name].dtype))
    for name, factor in factors.items():
        out[name] = (out[name] * factor).astype(out[name].dtype)
    return out
```

```python
from collections import namedtuple
from contextlib import ExitStack

import numpy as np

import concourse.bass as bass
from concourse import mybir

ALU = mybir.AluOpType
ACT = mybir.ActivationFunctionType
AX_X = mybir.AxisListType.X
F32 = mybir.dt.float32
F32R = mybir.dt.float32r

P = 128
G = 2
RING = 4
EPS = 1e-5
SLOPE = 0.2
TINY = 1e-12


class Step(namedtuple("Step", "base j pairs peeled")):

    def has(self, off):
        return not self.peeled or 0 <= self.base + self.j + off < self.pairs

    def pair(self, off):
        return self.base + (self.j + off)

    def slot(self, off):
        return (self.j + off) % RING

    def done(self, off):
        return self.base + (self.j + off + 1)

    def landed(self, off):
        return self.base * (16 // RING) + 16 * ((self.j + off) // RING + 1)

    def stat(self, back=0):
        return self.base + (self.j + 3 - back)

    def is_first(self):
        return self.peeled and self.base + self.j == FIRST


FIRST = -2


def over_steps(eng, pairs, step):
    last = pairs + 3
    lo, hi = RING, (pairs - 3) // RING * RING
    for s in range(FIRST, lo):
        step(Step(s // RING * RING, s % RING, pairs, True))
    with eng.Fori(lo // RING, hi // RING) as turn:
        for j in range(RING):
            step(Step(turn * RING, j, pairs, False))
    for s in range(hi, last):
        step(Step(s // RING * RING, s % RING, pairs, True))


def build(nc, x, adj2, wqk_t, wv_t, w1v_t, w1_bv, w1_aw, w1_ab, w1_wk, w1_bk, out):
    B, N, D = x.shape
    E2 = wqk_t.shape[1]
    E = E2 // 2
    K = w1_wk.shape[0]
    PAIRS = B // G
    C = D // P
    assert N == P and D == 2 * P and E2 == P and K == 3 and B % (G * RING) == 0
    QKV = E2 + D
    PS = D + 2
    SJ, SI = D, D + 1
    SCORE = 1.0 / float(E) ** 0.5

    x_pairs = x.rearrange("(p g) n d -> p n g d", g=G)
    out_pairs = out.rearrange("(p g) n d -> p n g d", g=G)
    adj_pairs = adj2.rearrange("(p g) n t m -> p n g (t m)", g=G)

    with ExitStack() as ctx:
        def sb(name, shape, dt=F32):
            return ctx.enter_context(nc.sbuf_tensor(name, shape, dt))

        def ps(name, shape):
            return ctx.enter_context(nc.psum_tensor(name, shape, F32))

        def sem(name):
            return ctx.enter_context(nc.semaphore(name))

        ident = sb("ident", [P, P])
        eps_c = sb("eps_c", [P, 4])
        mhalf = sb("mhalf", [P, 4])
        zero_c = sb("zero_c", [P, G])
        slope_c = sb("slope_c", [P, G])
        ones_f = sb("ones_f", [64, P])
        ones_r = sb("ones_r", [64, P], F32R)
        w0_f = sb("w0_f", [P, C, QKV])
        w2_f = sb("w2_f", [P, C, PS])
        w01_f = sb("w01_f", [P, C, 2 * D])
        w0_hi, w0_lo = sb("w0_hi", [P, C, QKV], F32R), sb("w0_lo", [P, C, QKV], F32R)
        w2_hi, w2_lo = sb("w2_hi", [P, C, PS], F32R), sb("w2_lo", [P, C, PS], F32R)
        w01_hi, w01_lo = sb("w01_hi", [P, C, 2 * D], F32R), sb("w01_lo", [P, C, 2 * D], F32R)
        wvt_f = sb("wvt_f", [P, C, D])
        aw_f = sb("aw_f", [P, C, 2])
        bv_f = sb("bv_f", [P, C])
        ab_f = sb("ab_f", [P, 1])
        bk_f = sb("bk_f", [64, D])
        bk_r = sb("bk_r", [64, D], F32R)
        e_const = sb("e_const", [P, 1])
        e_part = sb("e_part", [P, 2])

        xs = sb("xs", [P, RING, G, D])
        adjs = sb("adjs", [P, RING, G, 2 * N])
        x1s = sb("x1s", [P, RING, G, D])
        qkvs = sb("qkvs", [P, 2, G, QKV])

        stats = sb("stats", [P, 2, G, 6])
        carrier = sb("carrier", [P, 1])
        mv = sb("mv", [P, 2, G, 2])
        varq = sb("varq", [P, 4])
        rstd = sb("rstd", [P, 4])
        mr = sb("mr", [P, G])
        nmr = sb("nmr", [P, G])
        xn0, xn1 = sb("xn0", [P, G, D]), sb("xn1", [P, G, D])
        h0_hi, h0_lo = sb("h0_hi", [P, C, G, N], F32R), sb("h0_lo", [P, C, G, N], F32R)
        h1_hi, h1_lo = sb("h1_hi", [P, C, G, N], F32R), sb("h1_lo", [P, C, G, N], F32R)
        qak = sb("qak", [P, G, E])
        wcol = sb("wcol", [P, P])
        wmax, wbias = sb("wmax", [G, 1]), sb("wbias", [G, 1])
        wexp = sb("wexp", [G, N])
        wden, wrec = sb("wden", [G, 1]), sb("wrec", [G, 1])
        wnorm = sb("wnorm", [P, N])
        wsm = sb("wsm", [P, G])
        p2s = sb("p2s", [P, G, PS])
        b1, b2 = sb("b1", [P, G]), sb("b2", [P, G])
        e1, e2, emax = sb("e1", [P, G, N]), sb("e2", [P, G, N]), sb("emax", [P, G, N])
        alpha, tnat, tts = sb("alpha", [P, G, N]), sb("tnat", [P, G, N]), sb("tts", [P, G, N])
        rsum, rsum1, rinv = sb("rsum", [P, G]), sb("rsum1", [P, G]), sb("rinv", [P, G])
        us = sb("us", [P, G, D])

        A = ps("A", [P, G, 512])
        AK = QKV
        CC = ps("CC", [P, G, 512])
        CS, CW = PS, 512 - N
        DD = ps("DD", [P, G, 512])
        T0 = ps("T0", [P, 512])
        T1 = ps("T1", [P, 512])
        T0h = T0[:, :].rearrange("p (c g n) -> p c g n", c=C, g=G)
        T1h = T1[:, :].rearrange("p (c g n) -> p c g n", c=C, g=G)
        T0t = T0[:, 0:G * N].rearrange("p (g n) -> p g n", g=G)

        x_in = [sem(f"x_in{r}") for r in range(RING)]
        adj_in = [sem(f"adj_in{r}") for r in range(RING)]
        out_done = [sem(f"out_done{r}") for r in range(RING)]
        w_in = sem("w_in")
        consts, consts2 = sem("consts"), sem("consts2")
        wij_ready, w_split = sem("wij_ready"), sem("w_split")
        stats_x, stats_x1, mv_ready = sem("stats_x"), sem("stats_x1"), sem("mv_ready")
        var_ready, rstd_raw, mr_ready, rstd_ready = (sem("var_ready"), sem("rstd_raw"), sem("mr_ready"),
                                                     sem("rstd_ready"))
        xn0_ready, tr0_done, h0_hi_ready, h0_lo_ready = (sem("xn0_ready"), sem("tr0_done"), sem("h0_hi_ready"),
                                                         sem("h0_lo_ready"))
        qkv_done, qkv_saved, adjk_done, w_ready = (sem("qkv_done"), sem("qkv_saved"), sem("adjk_done"),
                                                   sem("w_ready"))
        wt_done, wmax_ready, wbias_ready, wexp_ready = (sem("wt_done"), sem("wmax_ready"), sem("wbias_ready"),
                                                        sem("wexp_ready"))
        wrec_ready, wnorm_ready, wb_done, wsm_ready = (sem("wrec_ready"), sem("wnorm_ready"), sem("wb_done"),
                                                       sem("wsm_ready"))
        x1_ready, xn1_ready, tr1_done, h1_hi_ready, h1_lo_ready = (
            sem("x1_ready"), sem("xn1_ready"), sem("tr1_done"), sem("h1_hi_ready"), sem("h1_lo_ready"))
        p2_done, p2_saved, sjt_done, b1_ready, bias_ready, exps_ready = (
            sem("p2_done"), sem("p2_saved"), sem("sjt_done"), sem("b1_ready"), sem("bias_ready"), sem("exps_ready"))
        emax_ready, alpha_ready, rsum1_ready, rinv_ready, t_ready = (
            sem("emax_ready"), sem("alpha_ready"), sem("rsum1_ready"), sem("rinv_ready"), sem("t_ready"))
        tt_done, tt_saved, u_done, u_saved, h_done, y_ready = (
            sem("tt_done"), sem("tt_saved"), sem("u_done"), sem("u_saved"), sem("h_done"), sem("y_ready"))

        block = ctx.enter_context(nc.Block())
        WEIGHT_LOADS = 11

        @block.sync
        def _(sp):
            def load_x(pair, slot):
                sp.dma_start(xs[:, slot], x_pairs[pair]).then_inc(x_in[slot], 16)

            def load_adj(pair, slot):
                sp.dma_start(adjs[:, slot], adj_pairs[pair]).then_inc(adj_in[slot], 16)

            load_x(0, 0)
            sp.dma_start(w0_f[:, :, 0:E2], wqk_t.rearrange("(c p) e -> p c e", p=P)).then_inc(w_in, 16)
            sp.dma_start(w0_f[:, :, E2:QKV], wv_t.rearrange("(c p) e -> p c e", p=P)).then_inc(w_in, 16)
            load_x(1, 1)
            load_adj(0, 0)
            sp.dma_start(wvt_f[:, :, :], w1v_t.rearrange("(c p) e -> p c e", p=P)).then_inc(w_in, 16)
            sp.dma_start(aw_f[:, :, :], w1_aw.rearrange("(c p) t -> p c t", p=P)).then_inc(w_in, 16)
            sp.dma_start(bv_f[:, :], w1_bv[:, :]).then_inc(w_in, 16)
            sp.dma_start(ab_f[:, :], w1_ab.rearrange("(a o) -> a o", a=1).broadcast_to([P, 1])).then_inc(w_in, 16)
            wk_v = w1_wk.rearrange("k (c p) e -> k p c e", p=P)
            sp.dma_start(w2_f[:, :, 0:D], wk_v[2]).then_inc(w_in, 16)
            for k in range(2):
                sp.dma_start(w01_f[:, :, k * D:(k + 1) * D], wk_v[k]).then_inc(w_in, 16)
            sp.wait_ge(consts2, 1)
            for r in (0, 32):
                sp.dma_start(bk_f[r:r + K, :], w1_bk[:, :]).then_inc(w_in, 16)
            load_x(2, 2)
            load_adj(1, 1)

            def step(st):
                if st.has(3) and st.has(0):
                    if st.has(-1):
                        sp.wait_ge(x1_ready, st.done(-1))
                    load_x(st.pair(3), st.slot(3))
                if st.has(-3):
                    sp.wait_ge(y_ready, st.done(-3))
                    sp.dma_start(out_pairs[st.pair(-3)], x1s[:, st.slot(-3)]).then_inc(out_done[st.slot(-3)], 16)
                if st.has(2) and st.has(0):
                    if st.has(-2):
                        sp.wait_ge(alpha_ready, st.done(-2))
                    load_adj(st.pair(2), st.slot(2))

            over_steps(sp, PAIRS, step)
            for r in range(RING):
                sp.wait_ge(out_done[r], 16 * (PAIRS // RING))

        @block.gpsimd
        def _(pool):
            pool.memset(ident[:, :], 0.0).then_inc(consts, 1)
            pool.wait_ge(consts, 1)
            pool.affine_select(out=ident[:, :], in_=ident[:, :], compare_op=ALU.not_equal, fill=1.0, base=0,
                               pattern=[[-1, P]], channel_multiplier=1).then_inc(consts, 1)
            pool.memset(eps_c[:, :], EPS).then_inc(consts, 1)
            pool.memset(mhalf[:, :], -0.5).then_inc(consts, 1)
            pool.memset(zero_c[:, :], 0.0).then_inc(consts, 1)
            pool.memset(slope_c[:, :], SLOPE).then_inc(consts, 1)
            pool.wait_ge(consts, 6)

            def step(st):
                if st.has(-2):
                    pool.wait_ge(p2_saved, st.done(-2))
                    if st.peeled and st.pair(-2) == 0:
                        pool.wait_ge(wij_ready, 3)
                    pool.tensor_tensor(out=b1[:, :], in0=p2s[:, :, SI], in1=e_const[:, :].broadcast_to([P, G]),
                                       op=ALU.add).then_inc(b1_ready, 1)
                    pool.wait_ge(b1_ready, st.done(-2))
                    pool.tensor_tensor(out=b2[:, :], in0=b1[:, :], in1=slope_c[:, :],
                                       op=ALU.mult).then_inc(bias_ready, 1)
                if st.has(2) or st.has(-1):
                    if st.has(1):
                        pool.wait_ge(xn0_ready, st.done(1))
                    pool.wait_ge(mv_ready, st.stat())
                    pool.tensor_tensor(out=varq[:, :], in0=mv[:, :, :, 1].rearrange("p l g -> p (l g)"),
                                       in1=eps_c[:, :], op=ALU.add).then_inc(var_ready, 1)
                    pool.wait_ge(var_ready, st.stat())
                    pool.tensor_tensor(out=rstd[:, :], in0=varq[:, :], in1=mhalf[:, :],
                                       op=ALU.pow).then_inc(rstd_raw, 1)
                    pool.wait_ge(rstd_raw, st.stat())
                    pool.tensor_tensor(out=mr[:, :], in0=mv[:, 0, :, 0], in1=rstd[:, 0:G],
                                       op=ALU.mult).then_inc(mr_ready, 1)
                    pool.wait_ge(mr_ready, st.stat())
                    pool.tensor_tensor(out=nmr[:, :], in0=zero_c[:, :], in1=mr[:, :],
                                       op=ALU.subtract).then_inc(rstd_ready, 1)

            over_steps(pool, PAIRS, step)

        @block.scalar
        def _(act):
            def step(st):
                if st.has(1):
                    act.wait_ge(rstd_ready, st.stat(1))
                    if st.has(0):
                        act.wait_ge(tr0_done, st.done(0))
                    for g in range(G):
                        last = act.activation(xn0[:, g], xs[:, st.slot(1), g], ACT.Identity,
                                              bias=nmr[:, g:g + 1], scale=rstd[:, g:g + 1])
                    last.then_inc(xn0_ready, 1)
                if st.has(-3):
                    act.wait_ge(rinv_ready, st.done(-3))
                    for g in range(G):
                        last = act.activation(tnat[:, g], alpha[:, g], ACT.Copy, scale=rinv[:, g:g + 1])
                    last.then_inc(t_ready, 1)
                if st.has(-2):
                    act.wait_ge(tr1_done, st.done(-2))
                    act.activation(h1_hi[:, :, :, :], T1h, ACT.Relu).then_inc(h1_hi_ready, 1)
                if st.has(-3):
                    act.wait_ge(tt_done, st.done(-3))
                    act.activation(tts[:, :, :], T0t, ACT.Copy).then_inc(tt_saved, 1)
                if st.has(-1):
                    act.wait_ge(wbias_ready, st.done(-1))
                    act.activation(wexp[:, :], CC[0:G, 0, CW:CW + N], ACT.Exp, bias=wbias[:, :], scale=SCORE,
                                   accum_out=wden[:, :]).then_inc(wexp_ready, 1)
                if st.has(0):
                    act.wait_ge(qkv_done, st.done(0))
                    act.activation(qkvs[:, st.j % 2], A[:, :, 0:QKV], ACT.Copy).then_inc(qkv_saved, 1)
                if st.has(-3):
                    act.wait_ge(u_done, st.done(-3))
                    act.activation(us[:, :, :], DD[:, :, D:2 * D], ACT.Copy).then_inc(u_saved, 1)
                if st.has(-2):
                    act.wait_ge(p2_done, st.done(-2))
                    act.activation(p2s[:, :, :], CC[:, :, 0:PS], ACT.Copy).then_inc(p2_saved, 1)
                if st.has(1):
                    act.wait_ge(tr0_done, st.done(1))
                    act.activation(h0_hi[:, :, :, :], T0h, ACT.Relu).then_inc(h0_hi_ready, 1)
                if st.has(-2):
                    act.wait_ge(sjt_done, st.done(-2))
                    act.wait_ge(bias_ready, st.done(-2))
                    for g in range(G):
                        act.activation(e1[:, g], CC[:, g, CS:CS + N], ACT.Exp, bias=b1[:, g:g + 1])
                        last = act.activation(e2[:, g], CC[:, g, CS:CS + N], ACT.Exp, bias=b2[:, g:g + 1],
                                              scale=SLOPE)
                    last.then_inc(exps_ready, 1)

            over_steps(act, PAIRS, step)

        @block.vector
        def _(dve):
            dve.memset(bk_f[:, :], 0.0).then_inc(consts2, 1)
            dve.memset(ones_f[:, :], 1.0).then_inc(consts2, 1)
            dve.memset(mv[:, :, :, :], 1.0).then_inc(consts2, 1)
            dve.memset(wcol[:, :], 0.0).then_inc(consts2, 1)
            dve.memset(wnorm[:, :], 0.0).then_inc(consts2, 1)
            dve.wait_ge(consts2, 5)
            dve.tensor_copy(out=ones_r[:, :], in_=ones_f[:, :]).then_inc(consts2, 1)

            def split(hi, lo, full, count):
                dve.tensor_copy(out=hi, in_=full).then_inc(w_split, 1)
                dve.wait_ge(w_split, count)
                dve.tensor_tensor(out=lo, in0=full, in1=hi.bitcast(F32), op=ALU.subtract).then_inc(w_split, 1)

            def split_weights():
                dve.wait_ge(w_in, 16 * WEIGHT_LOADS)
                split(w0_hi[:, :, :], w0_lo[:, :, :], w0_f[:, :, :], 1)
                split(w01_hi[:, :, :], w01_lo[:, :, :], w01_f[:, :, :], 3)
                dve.tensor_copy(out=bk_r[:, :], in_=bk_f[:, :]).then_inc(w_split, 1)
                dve.wait_ge(w_split, 5)
                dve.tensor_tensor(out=bk_r[32:32 + K, :], in0=bk_f[32:32 + K, :],
                                  in1=bk_r[32:32 + K, :].bitcast(F32), op=ALU.subtract).then_inc(w_split, 1)
                dve.wait_ge(wij_ready, 1)
                dve.tensor_copy(out=w2_f[:, :, D:PS], in_=DD[:, 0, 0:2 * C].rearrange("p (c t) -> p c t", c=C)
                                ).then_inc(w_split, 1)
                dve.tensor_copy(out=e_part[:, :], in_=DD[:, 0, 2 * C:2 * C + 2]).then_inc(w_split, 1)
                dve.wait_ge(w_split, 8)
                dve.tensor_tensor(out=e_const[:, :], in0=e_part[:, 0:1], in1=e_part[:, 1:2],
                                  op=ALU.add).then_inc(wij_ready, 1)
                dve.wait_ge(wij_ready, 2)
                dve.tensor_tensor(out=e_const[:, :], in0=e_const[:, :], in1=ab_f[:, :],
                                  op=ALU.add).then_inc(wij_ready, 1)
                split(w2_hi[:, :, :], w2_lo[:, :, :], w2_f[:, :, :], 9)

            def step(st):
                if st.peeled and st.pair(0) == 0:
                    split_weights()
                if st.has(-1):
                    dve.wait_ge(wt_done, st.done(-1))
                    dve.reduce_max(wmax[:, :], CC[0:G, 0, CW:CW + N], AX_X).then_inc(wmax_ready, 1)
                    dve.wait_ge(wmax_ready, st.done(-1))
                    dve.tensor_scalar(out=wbias[:, :], in0=wmax[:, :], scalar1=-SCORE, scalar2=None,
                                      op0=ALU.mult).then_inc(wbias_ready, 1)
                if st.has(-2):
                    dve.wait_ge(h1_hi_ready, st.done(-2))
                    dve.scalar_tensor_tensor(out=h1_lo[:, :, :, :].rearrange("p c g n -> p (c g n)"), in0=T1[:, :],
                                             scalar=0.0,
                                             in1=h1_hi[:, :, :, :].rearrange("p c g n -> p (c g n)").bitcast(F32),
                                             op0=ALU.max, op1=ALU.subtract).then_inc(h1_lo_ready, 1)
                if st.has(-1):
                    dve.wait_ge(wexp_ready, st.done(-1))
                    dve.reciprocal(out=wrec[:, :], in_=wden[:, :]).then_inc(wrec_ready, 1)
                    dve.wait_ge(wrec_ready, st.done(-1))
                    dve.tensor_scalar(out=wnorm[0:G, :], in0=wexp[:, :], scalar1=wrec[:, :], scalar2=None,
                                      op0=ALU.mult).then_inc(wnorm_ready, 1)
                if st.has(2):
                    if not st.is_first():
                        dve.wait_ge(mv_ready, st.stat(1))
                    dve.wait_ge(x_in[st.slot(2)], st.landed(2))
                    for g in range(G):
                        last = dve.bn_stats(out=stats[:, 0, g], in_=xs[:, st.slot(2), g])
                    last.then_inc(stats_x, 1)
                if st.has(-1):
                    dve.wait_ge(wb_done, st.done(-1))
                    dve.tensor_copy(out=wsm[:, :], in_=CC[:, 1, CW:CW + G]).then_inc(wsm_ready, 1)
                    if st.has(-5):
                        dve.wait_ge(out_done[st.slot(-5)], st.landed(-5))
                    dve.wait_ge(wsm_ready, st.done(-1))
                    for g in range(G):
                        last = dve.scalar_tensor_tensor(out=x1s[:, st.slot(-1), g], in0=qkvs[:, (st.j - 1) % 2, g, E2:QKV],
                                                        scalar=wsm[:, g:g + 1], in1=xs[:, st.slot(-1), g],
                                                        op0=ALU.mult, op1=ALU.add)
                    last.then_inc(x1_ready, 1)
                    dve.wait_ge(x1_ready, st.done(-1))
                    for g in range(G):
                        last = dve.bn_stats(out=stats[:, 1, g], in_=x1s[:, st.slot(-1), g])
                    last.then_inc(stats_x1, 1)
                if st.has(2) or st.has(-1):
                    if not st.is_first():
                        dve.wait_ge(rstd_ready, st.stat(1))
                    if st.has(-1):
                        dve.wait_ge(stats_x1, st.done(-1))
                    else:
                        dve.wait_ge(stats_x, st.done(2))
                    dve.memset(carrier[:, :], 0.0)
                    for layer in ([0] if st.has(2) else []) + ([1] if st.has(-1) else []):
                        for g in range(G):
                            last = dve.bn_aggr(out=mv[:, layer, g], in_=stats[:, layer, g])
                    last.then_inc(mv_ready, 1)
                if st.has(-3):
                    dve.wait_ge(h_done, st.done(-3))
                    dve.scalar_tensor_tensor(out=x1s[:, st.slot(-3)], in0=DD[:, :, 0:D], scalar=0.0,
                                             in1=x1s[:, st.slot(-3)], op0=ALU.max, op1=ALU.add).then_inc(y_ready, 1)
                if st.has(0):
                    dve.wait_ge(adjk_done, st.done(0))
                    for g in range(G):
                        last = dve.scalar_tensor_tensor(out=qak[:, g], in0=A[:, g, AK:AK + E], scalar=1.0,
                                                        in1=qkvs[:, st.j % 2, g, 0:E], op0=ALU.mult, op1=ALU.mult,
                                                        accum_out=wcol[:, g:g + 1])
                    last.then_inc(w_ready, 1)
                if st.has(1):
                    dve.wait_ge(h0_hi_ready, st.done(1))
                    dve.scalar_tensor_tensor(out=h0_lo[:, :, :, :].rearrange("p c g n -> p (c g n)"), in0=T0[:, :],
                                             scalar=0.0,
                                             in1=h0_hi[:, :, :, :].rearrange("p c g n -> p (c g n)").bitcast(F32),
                                             op0=ALU.max, op1=ALU.subtract).then_inc(h0_lo_ready, 1)
                if st.has(-1):
                    dve.wait_ge(rstd_ready, st.stat())
                    for g in range(G):
                        last = dve.tensor_scalar(out=xn1[:, g], in0=x1s[:, st.slot(-1), g], scalar1=mv[:, 1, g, 0:1],
                                                 scalar2=rstd[:, G + g:G + g + 1], op0=ALU.subtract, op1=ALU.mult)
                    last.then_inc(xn1_ready, 1)
                if st.has(-2):
                    dve.wait_ge(exps_ready, st.done(-2))
                    dve.tensor_tensor(out=emax[:, :, :], in0=e1[:, :, :], in1=e2[:, :, :],
                                      op=ALU.max).then_inc(emax_ready, 1)
                    if st.has(-3):
                        dve.wait_ge(t_ready, st.done(-3))
                    dve.wait_ge(adj_in[st.slot(-2)], st.landed(-2))
                    dve.wait_ge(emax_ready, st.done(-2))
                    for g in range(G):
                        last = dve.scalar_tensor_tensor(out=alpha[:, g], in0=emax[:, g], scalar=1.0,
                                                        in1=adjs[:, st.slot(-2), g, N:2 * N], op0=ALU.mult,
                                                        op1=ALU.mult, accum_out=rsum[:, g:g + 1])
                    last.then_inc(alpha_ready, 1)
                    dve.wait_ge(alpha_ready, st.done(-2))
                    dve.tensor_scalar(out=rsum1[:, :], in0=rsum[:, :], scalar1=TINY, scalar2=None,
                                      op0=ALU.add).then_inc(rsum1_ready, 1)
                    dve.wait_ge(rsum1_ready, st.done(-2))
                    dve.reciprocal(out=rinv[:, :], in_=rsum1[:, :]).then_inc(rinv_ready, 1)

            over_steps(dve, PAIRS, step)

        @block.tensor
        def _(pe):
            def weigh(out_, g, h_hi, h_lo, w_hi, w_lo, lo_ready, count, stop=True):
                for c in range(C):
                    for n, w in enumerate((w_hi, w_lo)):
                        nc.tensor.matmul(out_, h_hi[:, c, g], w[:, c], start=(c == 0 and n == 0), stop=False)
                if lo_ready is not None:
                    pe.wait_ge(lo_ready, count)
                for c in range(C):
                    last = nc.tensor.matmul(out_, h_lo[:, c, g], w_hi[:, c], start=False, stop=stop and c == C - 1)
                return last

            def transpose_h(out_, src):
                for c in range(C):
                    for g in range(G):
                        last = nc.tensor.transpose(out_[:, c, g], src[:, g, c * P:(c + 1) * P], ident[:, :])
                return last

            def fold_attention_weights():
                for c in range(C):
                    for k in range(C):
                        nc.tensor.matmul(DD[:, 0, 2 * c:2 * c + 2], wvt_f[:, k, c * P:(c + 1) * P], aw_f[:, k],
                                         start=(k == 0), stop=(k == C - 1))
                for k in range(C):
                    last = nc.tensor.matmul(DD[:, 0, 2 * C:2 * C + 2], bv_f[:, k:k + 1].broadcast_to([P, P]), aw_f[:, k],
                                            start=(k == 0), stop=(k == C - 1))
                last.then_inc(wij_ready, 1)

            pe.wait_ge(w_in, 16 * WEIGHT_LOADS)
            fold_attention_weights()
            pe.wait_ge(consts, 6)
            pe.wait_ge(consts2, 6)

            def step(st):
                if st.has(0):
                    pe.wait_ge(h0_hi_ready, st.done(0))
                    if st.has(-1):
                        pe.wait_ge(w_ready, st.done(-1))
                    elif st.peeled:
                        pe.wait_ge(w_split, 10)
                    weigh(A[:, 0, 0:QKV], 0, h0_hi, h0_lo, w0_hi, w0_lo, h0_lo_ready, st.done(0))
                elif st.has(-1):
                    pe.wait_ge(w_ready, st.done(-1))
                if st.has(-2):
                    pe.wait_ge(xn1_ready, st.done(-2))
                    transpose_h(T1h, xn1).then_inc(tr1_done, 1)
                if st.has(-1):
                    if st.has(-3):
                        pe.wait_ge(exps_ready, st.done(-3))
                    nc.tensor.transpose(CC[:, 0, CW:CW + N], wcol[:, :], ident[:, :]).then_inc(wt_done, 1)
                if st.has(-3):
                    pe.wait_ge(t_ready, st.done(-3))
                    for g in range(G):
                        last = nc.tensor.transpose(T0t[:, g], tnat[:, g], ident[:, :])
                    last.then_inc(tt_done, 1)
                if st.has(0):
                    weigh(A[:, 1, 0:QKV], 1, h0_hi, h0_lo, w0_hi, w0_lo, None, 0).then_inc(qkv_done, 1)
                if st.has(-3):
                    pe.wait_ge(tt_saved, st.done(-3))
                    for g in range(G):
                        last = nc.tensor.matmul(DD[:, g, D:2 * D], tts[:, g], p2s[:, g, 0:D], start=False, stop=True)
                    last.then_inc(u_done, 1)
                if st.has(-1):
                    pe.wait_ge(wnorm_ready, st.done(-1))
                    nc.tensor.matmul(CC[:, 1, CW:CW + G], wnorm[:, :], ident[:, 0:G], start=True,
                                     stop=True).then_inc(wb_done, 1)
                if st.has(-2):
                    pe.wait_ge(h1_hi_ready, st.done(-2))
                    weigh(CC[:, 0, 0:PS], 0, h1_hi, h1_lo, w2_hi, w2_lo, h1_lo_ready, st.done(-2))
                    if st.has(-1):
                        pe.wait_ge(wsm_ready, st.done(-1))
                    weigh(CC[:, 1, 0:PS], 1, h1_hi, h1_lo, w2_hi, w2_lo, None, 0).then_inc(p2_done, 1)
                if st.has(-3):
                    pe.wait_ge(u_saved, st.done(-3))
                    for g in range(G):
                        last = nc.tensor.matmul(DD[:, g, 0:D], tts[:, g], us[:, g], start=False, stop=True,
                                                skip_group_check=True)
                    last.then_inc(h_done, 1)
                if st.has(0):
                    pe.wait_ge(adj_in[st.slot(0)], st.landed(0))
                    pe.wait_ge(qkv_saved, st.done(0))
                    for g in range(G):
                        last = nc.tensor.matmul(A[:, g, AK:AK + E], adjs[:, st.slot(0), g, 0:N],
                                                qkvs[:, st.j % 2, g, E:E2], start=True, stop=True)
                    last.then_inc(adjk_done, 1)
                if st.has(1):
                    pe.wait_ge(xn0_ready, st.done(1))
                    transpose_h(T0h, xn0).then_inc(tr0_done, 1)
                if st.has(-2):
                    pe.wait_ge(p2_saved, st.done(-2))
                    for g in range(G):
                        last = nc.tensor.transpose(CC[:, g, CS:CS + N], p2s[:, g, SJ:SJ + 1].broadcast_to([P, P]),
                                                   ident[:, :])
                    last.then_inc(sjt_done, 1)
                    if st.has(-3):
                        pe.wait_ge(y_ready, st.done(-3))
                    for g in range(G):
                        weigh(DD[:, g], g, h1_hi, h1_lo, w01_hi, w01_lo, None, 0, stop=False)
                        nc.tensor.matmul(DD[:, g, 0:D], ones_r[:, :], bk_r[:, :], start=False, stop=False)

            over_steps(pe, PAIRS, step)


def kernel(x, adj, L0_gnn_W_qk, L0_gnn_W_v, L1_gnn_Wv, L1_gnn_bv, L1_gnn_aw, L1_gnn_ab, L1_gnn_Wk, L1_gnn_bk):
    import concourse.bacc as bacc
    from concourse.bass_utils import run_bass_kernel_spmd

    nc = bacc.Bacc("TRN2", target_bir_lowering=False, num_devices=1)
    adj = np.asarray(adj)
    host = {
        "x": np.asarray(x),
        "adj2": np.stack([adj.transpose(0, 2, 1), adj], axis=2),
        "wqk_t": np.asarray(L0_gnn_W_qk).T,
        "wv_t": np.asarray(L0_gnn_W_v).T,
        "w1v_t": np.asarray(L1_gnn_Wv).T,
        "w1_bv": np.asarray(L1_gnn_bv).reshape(-1, P).T,
        "w1_aw": np.asarray(L1_gnn_aw).reshape(2, -1).T,
        "w1_ab": np.asarray(L1_gnn_ab),
        "w1_wk": np.asarray(L1_gnn_Wk),
        "w1_bk": np.asarray(L1_gnn_bk),
    }
    arrays, args = {}, []
    for name, a in host.items():
        arrays[f"{name}_dram"] = np.ascontiguousarray(a)
        args.append(nc.dram_tensor(f"{name}_dram", a.shape, mybir.dt.from_np(a.dtype), kind="ExternalInput").ap())
    args.append(nc.dram_tensor("out_dram", host["x"].shape, F32, kind="ExternalOutput").ap())
    build(nc, *args)
    result = run_bass_kernel_spmd(nc, [arrays], core_ids=[0])
    return result.results[0]["out_dram"]
```

```python
from collections import namedtuple
from contextlib import ExitStack

import numpy as np

import concourse.bass as bass
from concourse import mybir

ALU = mybir.AluOpType
ACT = mybir.ActivationFunctionType
AX_X = mybir.AxisListType.X
F32 = mybir.dt.float32
F32R = mybir.dt.float32r

P = 128
G = 2
RING = 4
EPS = 1e-5
SLOPE = 0.2
TINY = 1e-12


class Step(namedtuple("Step", "base j pairs peeled")):

    def has(self, off):
        return not self.peeled or 0 <= self.base + self.j + off < self.pairs

    def pair(self, off):
        return self.base + (self.j + off)

    def slot(self, off):
        return (self.j + off) % RING

    def done(self, off):
        return self.base + (self.j + off + 1)

    def stepped(self, back=0):
        return self.base + (self.j + 1 - FIRST - back)

    def landed(self, off):
        return self.base * (16 // RING) + 16 * ((self.j + off) // RING + 1)

    def at(self, number):
        return self.peeled and self.base + self.j == number


FIRST = -2


def over_steps(eng, pairs, step):
    last = pairs + 4
    lo, hi = 2 * RING, (pairs - 3) // RING * RING
    for s in range(FIRST, lo):
        step(Step(s // RING * RING, s % RING, pairs, True))
    with eng.Fori(lo // RING, hi // RING) as turn:
        for j in range(RING):
            step(Step(turn * RING, j, pairs, False))
    for s in range(hi, last):
        step(Step(s // RING * RING, s % RING, pairs, True))


def build(nc, x, adj2, wqk_t, wv_t, w1v_t, w1_bv, w1_aw, w1_ab, w1_wk, w1_bk, out):
    B, N, D = x.shape
    E2 = wqk_t.shape[1]
    E = E2 // 2
    K = w1_wk.shape[0]
    PAIRS = B // G
    C = D // P
    assert N == P and D == 2 * P and E2 == P and K == 3 and B % (G * RING) == 0
    QKV = E2 + D
    PS = D + 2
    SJ, SI = D, D + 1
    SCORE = 1.0 / float(E) ** 0.5

    x_pairs = x.rearrange("(p g) n d -> p n g d", g=G)
    out_pairs = out.rearrange("(p g) n d -> p n g d", g=G)
    adj_pairs = adj2.rearrange("(p g) n t m -> p n g (t m)", g=G)

    with ExitStack() as ctx:
        def sb(name, shape, dt=F32):
            return ctx.enter_context(nc.sbuf_tensor(name, shape, dt))

        def ps(name, shape):
            return ctx.enter_context(nc.psum_tensor(name, shape, F32))

        def sem(name):
            return ctx.enter_context(nc.semaphore(name))

        ident = sb("ident", [P, P])
        eps_c = sb("eps_c", [P, 2 * G])
        mhalf = sb("mhalf", [P, 2 * G])
        zero_c = sb("zero_c", [P, 2 * G])
        slope_c = sb("slope_c", [P, G])
        ones_f = sb("ones_f", [64, P])
        ones_r = sb("ones_r", [64, P], F32R)
        w0_f = sb("w0_f", [P, C, QKV])
        w2_f = sb("w2_f", [P, C, PS])
        w01_f = sb("w01_f", [P, C, 2 * D])
        w0_hi, w0_lo = sb("w0_hi", [P, C, QKV], F32R), sb("w0_lo", [P, C, QKV], F32R)
        w2_hi, w2_lo = sb("w2_hi", [P, C, PS], F32R), sb("w2_lo", [P, C, PS], F32R)
        w01_hi, w01_lo = sb("w01_hi", [P, C, 2 * D], F32R), sb("w01_lo", [P, C, 2 * D], F32R)
        wvt_f = sb("wvt_f", [P, C, D])
        aw_f = sb("aw_f", [P, C, 2])
        bv_f = sb("bv_f", [P, C])
        ab_f = sb("ab_f", [P, 1])
        bk_f = sb("bk_f", [64, D])
        bk_r = sb("bk_r", [64, D], F32R)
        e_const = sb("e_const", [P, 1])
        e_part, e_sum = sb("e_part", [P, 2]), sb("e_sum", [P, 1])

        xs = sb("xs", [P, RING, G, D])
        adjs = sb("adjs", [P, RING, G, 2 * N])
        x1s = sb("x1s", [P, RING, G, D])
        qkvs = sb("qkvs", [P, 2, G, QKV])

        stats = sb("stats", [P, 2, G, 6])
        carrier = sb("carrier", [P, 1])
        mv = sb("mv", [P, 2, G, 2])
        vareps, rstd = sb("vareps", [P, 2, G]), sb("rstd", [P, 2, G])
        mr, nmr = sb("mr", [P, 2, G]), sb("nmr", [P, 2, G])
        xn0, xn1 = sb("xn0", [P, G, D]), sb("xn1", [P, G, D])
        h0_hi, h0_lo = sb("h0_hi", [P, C, G, N], F32R), sb("h0_lo", [P, C, G, N], F32R)
        h1_hi, h1_lo = sb("h1_hi", [P, C, G, N], F32R), sb("h1_lo", [P, C, G, N], F32R)
        qak = sb("qak", [P, G, E])
        wcol = sb("wcol", [P, P])
        wmax, wbias = sb("wmax", [G, 1]), sb("wbias", [G, 1])
        wexp = sb("wexp", [P, N])
        wden, wrec = sb("wden", [G, 1]), sb("wrec", [G, 1])
        wdiag = sb("wdiag", [P, G])
        wsm = sb("wsm", [P, G])
        p2s = sb("p2s", [P, G, PS])
        p2_hi, p2_lo = sb("p2_hi", [P, G, D], F32R), sb("p2_lo", [P, G, D], F32R)
        b1, b2 = sb("b1", [P, G]), sb("b2", [P, G])
        e1, e2, emax = sb("e1", [P, G, N]), sb("e2", [P, G, N]), sb("emax", [P, G, N])
        alpha, tnat = sb("alpha", [P, G, N]), sb("tnat", [P, G, N])
        tt_hi, tt_lo = sb("tt_hi", [P, G, N], F32R), sb("tt_lo", [P, G, N], F32R)
        rsum, rsum1, rinv = sb("rsum", [P, G]), sb("rsum1", [P, G]), sb("rinv", [P, G])
        u_hi, u_lo = sb("u_hi", [P, G, D], F32R), sb("u_lo", [P, G, D], F32R)

        A = ps("A", [P, G, 512])
        AK = QKV
        CC = ps("CC", [P, G, 512])
        DD = ps("DD", [P, G, 512])
        T0 = ps("T0", [P, 512])
        T1 = ps("T1", [P, 512])
        T0h = T0[:, :].rearrange("p (c g n) -> p c g n", c=C, g=G)
        T1h = T1[:, :].rearrange("p (c g n) -> p c g n", c=C, g=G)
        T0t = T0[:, 0:G * N].rearrange("p (g n) -> p g n", g=G)

        x_in = [sem(f"x_in{r}") for r in range(RING)]
        adj_in = [sem(f"adj_in{r}") for r in range(RING)]
        out_done = [sem(f"out_done{r}") for r in range(RING)]
        w0_in, fold_in, w01_in, w2_in = sem("w0_in"), sem("fold_in"), sem("w01_in"), sem("w2_in")
        consts, consts2 = sem("consts"), sem("consts2")
        fold_done, e_const_ready, w_hi, w_lo = sem("fold_done"), sem("e_const_ready"), sem("w_hi"), sem("w_lo")
        bk_split, w2_ready = sem("bk_split"), sem("w2_ready")
        stats0_ready, stats1_ready, xn0_ready, xn1_ready = (
            sem("stats0_ready"), sem("stats1_ready"), sem("xn0_ready"), sem("xn1_ready"))
        mv_ready, vareps_ready, rstd_ready, mr_ready, norm_ready = (
            sem("mv_ready"), sem("vareps_ready"), sem("rstd_ready"), sem("mr_ready"), sem("norm_ready"))
        tr0_done, h0_hi_ready, h0_lo_ready = sem("tr0_done"), sem("h0_hi_ready"), sem("h0_lo_ready")
        tr1_done, h1_hi_ready, h1_lo_ready = sem("tr1_done"), sem("h1_hi_ready"), sem("h1_lo_ready")
        qkv_done, qkv_saved, adjk_done, w_ready = (sem("qkv_done"), sem("qkv_saved"), sem("adjk_done"),
                                                   sem("w_ready"))
        wt_done, wmax_ready, wbias_ready, wexp_ready = (sem("wt_done"), sem("wmax_ready"), sem("wbias_ready"),
                                                        sem("wexp_ready"))
        wrec_ready, wdiag_ready, wb_done, wsm_ready, x1_ready = (
            sem("wrec_ready"), sem("wdiag_ready"), sem("wb_done"), sem("wsm_ready"), sem("x1_ready"))
        p2_done, p2_saved, p2_hi_ready, p2_lo_ready = (sem("p2_done"), sem("p2_saved"), sem("p2_hi_ready"),
                                                       sem("p2_lo_ready"))
        sjt_done, b1_ready, bias_ready, exps_ready = (sem("sjt_done"), sem("b1_ready"), sem("bias_ready"),
                                                      sem("exps_ready"))
        emax_ready, alpha_ready, rsum1_ready, rinv_ready, t_ready = (
            sem("emax_ready"), sem("alpha_ready"), sem("rsum1_ready"), sem("rinv_ready"), sem("t_ready"))
        tt_done, tt_hi_ready, tt_lo_ready = sem("tt_done"), sem("tt_hi_ready"), sem("tt_lo_ready")
        u_done, u_hi_ready, u_lo_ready = sem("u_done"), sem("u_hi_ready"), sem("u_lo_ready")
        h_done = [sem(f"h_done{g}") for g in range(G)]
        y_ready = [sem(f"y_ready{g}") for g in range(G)]

        block = ctx.enter_context(nc.Block())

        @block.sync
        def _(sp):
            def load_x(pair, slot):
                sp.dma_start(xs[:, slot], x_pairs[pair]).then_inc(x_in[slot], 16)

            def load_adj(pair, slot):
                sp.dma_start(adjs[:, slot], adj_pairs[pair]).then_inc(adj_in[slot], 16)

            load_x(0, 0)
            sp.dma_start(w0_f[:, :, 0:E2], wqk_t.rearrange("(c p) e -> p c e", p=P)).then_inc(w0_in, 16)
            sp.dma_start(w0_f[:, :, E2:QKV], wv_t.rearrange("(c p) e -> p c e", p=P)).then_inc(w0_in, 16)
            load_x(1, 1)
            load_adj(0, 0)
            sp.dma_start(wvt_f[:, :, :], w1v_t.rearrange("(c p) e -> p c e", p=P)).then_inc(fold_in, 16)
            sp.dma_start(aw_f[:, :, :], w1_aw.rearrange("(c p) t -> p c t", p=P)).then_inc(fold_in, 16)
            sp.dma_start(bv_f[:, :], w1_bv[:, :]).then_inc(fold_in, 16)
            sp.dma_start(ab_f[:, :], w1_ab.rearrange("(a o) -> a o", a=1).broadcast_to([P, 1])).then_inc(fold_in, 16)
            load_x(2, 2)
            wk_v = w1_wk.rearrange("k (c p) e -> k p c e", p=P)
            sp.wait_ge(consts2, 1)
            for k in range(2):
                sp.dma_start(w01_f[:, :, k * D:(k + 1) * D], wk_v[k]).then_inc(w01_in, 16)
            for r in (0, 32):
                sp.dma_start(bk_f[r:r + K, :], w1_bk[:, :]).then_inc(w01_in, 16)
            sp.dma_start(w2_f[:, :, 0:D], wk_v[2]).then_inc(w2_in, 16)

            def step(st):
                if st.has(3) and st.has(0):
                    if st.has(-1):
                        sp.wait_ge(x1_ready, st.done(-1))
                    load_x(st.pair(3), st.slot(3))
                if st.has(-4):
                    sp.wait_ge(y_ready[G - 1], st.done(-4))
                    sp.dma_start(out_pairs[st.pair(-4)], x1s[:, st.slot(-4)]).then_inc(out_done[st.slot(-4)], 16)
                if st.has(1) and st.has(0):
                    if st.has(-3):
                        sp.wait_ge(alpha_ready, st.done(-3))
                    load_adj(st.pair(1), st.slot(1))

            over_steps(sp, PAIRS, step)
            for r in range(RING):
                sp.wait_ge(out_done[r], 16 * (PAIRS // RING))

        @block.gpsimd
        def _(pool):
            pool.memset(ident[:, :], 0.0).then_inc(consts, 1)
            pool.wait_ge(consts, 1)
            pool.affine_select(out=ident[:, :], in_=ident[:, :], compare_op=ALU.not_equal, fill=1.0, base=0,
                               pattern=[[-1, P]], channel_multiplier=1).then_inc(consts, 1)
            pool.memset(eps_c[:, :], EPS).then_inc(consts, 1)
            pool.memset(mhalf[:, :], -0.5).then_inc(consts, 1)
            pool.memset(zero_c[:, :], 0.0).then_inc(consts, 1)
            pool.memset(slope_c[:, :], SLOPE).then_inc(consts, 1)
            pool.wait_ge(consts, 6)

            def step(st):
                if st.has(2) or st.has(-2):
                    pool.wait_ge(mv_ready, st.stepped())
                    pool.tensor_tensor(out=vareps[:, :, :].rearrange("p l g -> p (l g)"),
                                       in0=mv[:, :, :, 1].rearrange("p l g -> p (l g)"),
                                       in1=eps_c[:, :], op=ALU.add).then_inc(vareps_ready, 1)
                if st.has(-3):
                    if st.at(3):
                        pool.wait_ge(e_const_ready, 3)
                    pool.wait_ge(p2_saved, st.done(-3))
                    pool.tensor_tensor(out=b1[:, :], in0=p2s[:, :, SI], in1=e_const[:, :].broadcast_to([P, G]),
                                       op=ALU.add).then_inc(b1_ready, 1)
                    pool.wait_ge(b1_ready, st.done(-3))
                    pool.tensor_tensor(out=b2[:, :], in0=b1[:, :], in1=slope_c[:, :],
                                       op=ALU.mult).then_inc(bias_ready, 1)
                if st.has(2) or st.has(-2):
                    if st.has(1):
                        pool.wait_ge(xn0_ready, st.done(1))
                    if st.has(-3):
                        pool.wait_ge(xn1_ready, st.done(-3))
                    pool.wait_ge(vareps_ready, st.stepped())
                    pool.tensor_tensor(out=rstd[:, :, :].rearrange("p l g -> p (l g)"),
                                       in0=vareps[:, :, :].rearrange("p l g -> p (l g)"),
                                       in1=mhalf[:, :], op=ALU.pow).then_inc(rstd_ready, 1)
                    pool.wait_ge(rstd_ready, st.stepped())
                    pool.tensor_tensor(out=mr[:, :, :].rearrange("p l g -> p (l g)"),
                                       in0=mv[:, :, :, 0].rearrange("p l g -> p (l g)"),
                                       in1=rstd[:, :, :].rearrange("p l g -> p (l g)"),
                                       op=ALU.mult).then_inc(mr_ready, 1)
                    pool.wait_ge(mr_ready, st.stepped())
                    pool.tensor_tensor(out=nmr[:, :, :].rearrange("p l g -> p (l g)"), in0=zero_c[:, :],
                                       in1=mr[:, :, :].rearrange("p l g -> p (l g)"),
                                       op=ALU.subtract).then_inc(norm_ready, 1)
                if st.has(-3):
                    pool.wait_ge(p2_hi_ready, st.done(-3))
                    pool.tensor_tensor(out=p2_lo[:, :, :], in0=p2s[:, :, 0:D], in1=p2_hi[:, :, :].bitcast(F32),
                                       op=ALU.subtract).then_inc(p2_lo_ready, 1)

            over_steps(pool, PAIRS, step)

        @block.scalar
        def _(act):
            def step(st):
                if st.at(FIRST):
                    act.wait_ge(w0_in, 32)
                    act.activation(w0_hi[:, :, :], w0_f[:, :, :], ACT.Copy).then_inc(w_hi, 1)
                if st.at(0):
                    act.wait_ge(w01_in, 64)
                    act.activation(w01_hi[:, :, :], w01_f[:, :, :], ACT.Copy).then_inc(w_hi, 1)
                if st.at(1):
                    act.wait_ge(w2_ready, 1)
                    act.activation(w2_hi[:, :, :], w2_f[:, :, :], ACT.Copy).then_inc(w_hi, 1)
                if st.has(-4):
                    act.wait_ge(rinv_ready, st.done(-4))
                    for g in range(G):
                        last = act.activation(tnat[:, g], alpha[:, g], ACT.Copy, scale=rinv[:, g:g + 1])
                    last.then_inc(t_ready, 1)
                if st.has(-3):
                    act.wait_ge(tr1_done, st.done(-3))
                    act.activation(h1_hi[:, :, :, :], T1h, ACT.Relu).then_inc(h1_hi_ready, 1)
                if st.has(-1):
                    act.wait_ge(wbias_ready, st.done(-1))
                    act.activation(wexp[0:G, :], CC[0:G, 1, 0:N], ACT.Exp, bias=wbias[:, :], scale=SCORE,
                                   accum_out=wden[:, :]).then_inc(wexp_ready, 1)
                if st.has(-4):
                    act.wait_ge(tt_done, st.done(-4))
                    act.activation(tt_hi[:, :, :], T0t, ACT.Copy).then_inc(tt_hi_ready, 1)
                if st.has(0):
                    act.wait_ge(qkv_done, st.done(0))
                    act.activation(qkvs[:, st.j % 2], A[:, :, 0:QKV], ACT.Copy).then_inc(qkv_saved, 1)
                if st.has(-4):
                    act.wait_ge(u_done, st.done(-4))
                    act.activation(u_hi[:, :, :], DD[:, :, D:2 * D], ACT.Copy).then_inc(u_hi_ready, 1)
                if st.has(1):
                    act.wait_ge(norm_ready, st.stepped(1))
                    for g in range(G):
                        last = act.activation(xn0[:, g], xs[:, st.slot(1), g], ACT.Identity,
                                              bias=nmr[:, 0, g:g + 1], scale=rstd[:, 0, g:g + 1])
                    last.then_inc(xn0_ready, 1)
                if st.has(-3):
                    act.wait_ge(p2_done, st.done(-3))
                    if st.has(-4):
                        act.wait_ge(p2_lo_ready, st.done(-4))
                    act.activation(p2s[:, :, :], CC[:, :, 0:PS], ACT.Copy).then_inc(p2_saved, 1)
                    act.activation(p2_hi[:, :, :], CC[:, :, 0:D], ACT.Copy).then_inc(p2_hi_ready, 1)
                if st.has(1):
                    act.wait_ge(tr0_done, st.done(1))
                    act.activation(h0_hi[:, :, :, :], T0h, ACT.Relu).then_inc(h0_hi_ready, 1)
                if st.has(-3):
                    act.wait_ge(bias_ready, st.done(-3))
                    act.wait_ge(sjt_done, st.done(-3))
                    for g in range(G):
                        act.activation(e1[:, g], A[:, g, 0:N], ACT.Exp, bias=b1[:, g:g + 1])
                        last = act.activation(e2[:, g], A[:, g, 0:N], ACT.Exp, bias=b2[:, g:g + 1], scale=SLOPE)
                    last.then_inc(exps_ready, 1)
                if st.has(-2):
                    act.wait_ge(norm_ready, st.stepped())
                    for g in range(G):
                        last = act.activation(xn1[:, g], x1s[:, st.slot(-2), g], ACT.Identity,
                                              bias=nmr[:, 1, g:g + 1], scale=rstd[:, 1, g:g + 1])
                    last.then_inc(xn1_ready, 1)

            over_steps(act, PAIRS, step)

        @block.vector
        def _(dve):
            dve.memset(bk_f[:, :], 0.0).then_inc(consts2, 1)
            dve.memset(ones_f[:, :], 1.0).then_inc(consts2, 1)
            dve.memset(wcol[:, :], 0.0).then_inc(consts2, 1)
            dve.memset(wexp[:, :], 0.0).then_inc(consts2, 1)
            dve.memset(wdiag[:, :], 0.0).then_inc(consts2, 1)
            dve.memset(mv[:, :, :, :], 1.0).then_inc(consts2, 1)
            dve.wait_ge(consts2, 6)
            dve.tensor_copy(out=ones_r[:, :], in_=ones_f[:, :]).then_inc(consts2, 1)

            def split_w0():
                dve.wait_ge(w_hi, 1)
                dve.tensor_tensor(out=w0_lo[:, :, :], in0=w0_f[:, :, :], in1=w0_hi[:, :, :].bitcast(F32),
                                  op=ALU.subtract).then_inc(w_lo, 1)

            def split_w01():
                dve.wait_ge(w_hi, 2)
                dve.tensor_tensor(out=w01_lo[:, :, :], in0=w01_f[:, :, :], in1=w01_hi[:, :, :].bitcast(F32),
                                  op=ALU.subtract).then_inc(w_lo, 1)
                dve.tensor_copy(out=bk_r[:, :], in_=bk_f[:, :]).then_inc(bk_split, 1)
                dve.wait_ge(bk_split, 1)
                dve.tensor_tensor(out=bk_r[32:32 + K, :], in0=bk_f[32:32 + K, :],
                                  in1=bk_r[32:32 + K, :].bitcast(F32), op=ALU.subtract).then_inc(bk_split, 1)
                dve.wait_ge(w2_in, 16)
                dve.wait_ge(fold_done, 1)
                dve.tensor_copy(out=w2_f[:, :, D:PS], in_=DD[:, 0, 0:2 * C].rearrange("p (c t) -> p c t", c=C)
                                ).then_inc(w2_ready, 1)
                dve.tensor_copy(out=e_part[:, :], in_=DD[:, 0, 2 * C:2 * C + 2]).then_inc(e_const_ready, 1)
                dve.wait_ge(e_const_ready, 1)
                dve.tensor_tensor(out=e_sum[:, :], in0=e_part[:, 0:1], in1=e_part[:, 1:2],
                                  op=ALU.add).then_inc(e_const_ready, 1)
                dve.wait_ge(e_const_ready, 2)
                dve.tensor_tensor(out=e_const[:, :], in0=e_sum[:, :], in1=ab_f[:, :],
                                  op=ALU.add).then_inc(e_const_ready, 1)

            def split_w2():
                dve.wait_ge(w_hi, 3)
                dve.tensor_tensor(out=w2_lo[:, :, :], in0=w2_f[:, :, :], in1=w2_hi[:, :, :].bitcast(F32),
                                  op=ALU.subtract).then_inc(w_lo, 1)

            def step(st):
                if st.has(2):
                    if st.has(1):
                        dve.wait_ge(mv_ready, st.stepped(1))
                    dve.wait_ge(x_in[st.slot(2)], st.landed(2))
                    for g in range(G):
                        last = dve.bn_stats(out=stats[:, 0, g], in_=xs[:, st.slot(2), g])
                    last.then_inc(stats0_ready, 1)
                if st.at(2):
                    split_w2()
                if st.has(-1):
                    dve.wait_ge(wt_done, st.done(-1))
                    dve.reduce_max(wmax[:, :], CC[0:G, 1, 0:N], AX_X).then_inc(wmax_ready, 1)
                    dve.wait_ge(wmax_ready, st.done(-1))
                    dve.tensor_scalar(out=wbias[:, :], in0=wmax[:, :], scalar1=-SCORE, scalar2=None,
                                      op0=ALU.mult).then_inc(wbias_ready, 1)
                if st.has(-3):
                    dve.wait_ge(h1_hi_ready, st.done(-3))
                    dve.scalar_tensor_tensor(out=h1_lo[:, :, :, :].rearrange("p c g n -> p (c g n)"), in0=T1[:, :],
                                             scalar=0.0,
                                             in1=h1_hi[:, :, :, :].rearrange("p c g n -> p (c g n)").bitcast(F32),
                                             op0=ALU.max, op1=ALU.subtract).then_inc(h1_lo_ready, 1)
                if st.has(-1):
                    dve.wait_ge(wexp_ready, st.done(-1))
                    dve.reciprocal(out=wrec[:, :], in_=wden[:, :]).then_inc(wrec_ready, 1)
                    dve.wait_ge(wrec_ready, st.done(-1))
                    dve.tensor_scalar(out=wdiag[0:G, :], in0=ident[0:G, 0:G], scalar1=wrec[:, :], scalar2=None,
                                      op0=ALU.mult).then_inc(wdiag_ready, 1)
                if st.has(-4):
                    dve.wait_ge(tt_hi_ready, st.done(-4))
                    dve.tensor_tensor(out=tt_lo[:, :, :], in0=T0t, in1=tt_hi[:, :, :].bitcast(F32),
                                      op=ALU.subtract).then_inc(tt_lo_ready, 1)
                if st.has(-2):
                    if not st.has(2):
                        dve.wait_ge(mv_ready, st.stepped(1))
                    for g in range(G):
                        last = dve.bn_stats(out=stats[:, 1, g], in_=x1s[:, st.slot(-2), g])
                    last.then_inc(stats1_ready, 1)
                if st.has(-1):
                    dve.wait_ge(wb_done, st.done(-1))
                    dve.tensor_copy(out=wsm[:, :], in_=T1[:, 0:G]).then_inc(wsm_ready, 1)
                    if st.has(-5):
                        dve.wait_ge(out_done[st.slot(-5)], st.landed(-5))
                    dve.wait_ge(wsm_ready, st.done(-1))
                    for g in range(G):
                        last = dve.scalar_tensor_tensor(out=x1s[:, st.slot(-1), g],
                                                        in0=qkvs[:, (st.j - 1) % 2, g, E2:QKV],
                                                        scalar=wsm[:, g:g + 1], in1=xs[:, st.slot(-1), g],
                                                        op0=ALU.mult, op1=ALU.add)
                    last.then_inc(x1_ready, 1)
                if st.has(-4):
                    dve.wait_ge(u_hi_ready, st.done(-4))
                    dve.tensor_tensor(out=u_lo[:, :, :], in0=DD[:, :, D:2 * D], in1=u_hi[:, :, :].bitcast(F32),
                                      op=ALU.subtract).then_inc(u_lo_ready, 1)
                if st.has(2) or st.has(-2):
                    if not st.at(FIRST):
                        dve.wait_ge(norm_ready, st.stepped(1))
                    if st.has(-2):
                        dve.wait_ge(stats1_ready, st.done(-2))
                    else:
                        dve.wait_ge(stats0_ready, st.done(2))
                    dve.memset(carrier[:, :], 0.0)
                    for layer in ([0] if st.has(2) else []) + ([1] if st.has(-2) else []):
                        for g in range(G):
                            last = dve.bn_aggr(out=mv[:, layer, g], in_=stats[:, layer, g])
                    last.then_inc(mv_ready, 1)
                if st.has(0):
                    dve.wait_ge(adjk_done, st.done(0))
                    for g in range(G):
                        last = dve.scalar_tensor_tensor(out=qak[:, g], in0=A[:, g, AK:AK + E], scalar=1.0,
                                                        in1=qkvs[:, st.j % 2, g, 0:E], op0=ALU.mult, op1=ALU.mult,
                                                        accum_out=wcol[:, g:g + 1])
                    last.then_inc(w_ready, 1)
                if st.has(-4):
                    for g in range(G):
                        dve.wait_ge(h_done[g], st.done(-4))
                        dve.scalar_tensor_tensor(out=x1s[:, st.slot(-4), g], in0=DD[:, g, 0:D], scalar=0.0,
                                                 in1=x1s[:, st.slot(-4), g], op0=ALU.max,
                                                 op1=ALU.add).then_inc(y_ready[g], 1)
                if st.at(FIRST):
                    split_w0()
                if st.has(1):
                    dve.wait_ge(h0_hi_ready, st.done(1))
                    dve.scalar_tensor_tensor(out=h0_lo[:, :, :, :].rearrange("p c g n -> p (c g n)"), in0=T0[:, :],
                                             scalar=0.0,
                                             in1=h0_hi[:, :, :, :].rearrange("p c g n -> p (c g n)").bitcast(F32),
                                             op0=ALU.max, op1=ALU.subtract).then_inc(h0_lo_ready, 1)
                if st.has(-3):
                    dve.wait_ge(exps_ready, st.done(-3))
                    dve.tensor_tensor(out=emax[:, :, :], in0=e1[:, :, :], in1=e2[:, :, :],
                                      op=ALU.max).then_inc(emax_ready, 1)
                    if st.has(-4):
                        dve.wait_ge(t_ready, st.done(-4))
                    dve.wait_ge(adj_in[st.slot(-3)], st.landed(-3))
                    dve.wait_ge(emax_ready, st.done(-3))
                    for g in range(G):
                        last = dve.scalar_tensor_tensor(out=alpha[:, g], in0=emax[:, g], scalar=1.0,
                                                        in1=adjs[:, st.slot(-3), g, N:2 * N], op0=ALU.mult,
                                                        op1=ALU.mult, accum_out=rsum[:, g:g + 1])
                    last.then_inc(alpha_ready, 1)
                    dve.wait_ge(alpha_ready, st.done(-3))
                    dve.tensor_scalar(out=rsum1[:, :], in0=rsum[:, :], scalar1=TINY, scalar2=None,
                                      op0=ALU.add).then_inc(rsum1_ready, 1)
                    dve.wait_ge(rsum1_ready, st.done(-3))
                    dve.reciprocal(out=rinv[:, :], in_=rsum1[:, :]).then_inc(rinv_ready, 1)
                if st.at(0):
                    split_w01()

            over_steps(dve, PAIRS, step)

        @block.tensor
        def _(pe):
            def weigh(out_, g, h_hi, h_lo, w_hi_, w_lo_, stop=True):
                for c in range(C):
                    for n, w in enumerate((w_hi_, w_lo_)):
                        nc.tensor.matmul(out_, h_hi[:, c, g], w[:, c], start=(c == 0 and n == 0), stop=False)
                for c in range(C):
                    last = nc.tensor.matmul(out_, h_lo[:, c, g], w_hi_[:, c], start=False, stop=stop and c == C - 1)
                return last

            def propagate(out_, g, v_hi, v_lo, **group):
                nc.tensor.matmul(out_, tt_hi[:, g], v_hi[:, g], start=False, stop=False, **group)
                nc.tensor.matmul(out_, tt_lo[:, g], v_hi[:, g], start=False, stop=False, **group)
                return nc.tensor.matmul(out_, tt_hi[:, g], v_lo[:, g], start=False, stop=True, **group)

            def transpose_h(out_, src):
                for c in range(C):
                    for g in range(G):
                        last = nc.tensor.transpose(out_[:, c, g], src[:, g, c * P:(c + 1) * P], ident[:, :])
                return last

            def fold_attention_weights():
                pe.wait_ge(fold_in, 64)
                for c in range(C):
                    for k in range(C):
                        nc.tensor.matmul(DD[:, 0, 2 * c:2 * c + 2], wvt_f[:, k, c * P:(c + 1) * P], aw_f[:, k],
                                         start=(k == 0), stop=(k == C - 1))
                for k in range(C):
                    last = nc.tensor.matmul(DD[:, 0, 2 * C:2 * C + 2], bv_f[:, k:k + 1].broadcast_to([P, P]),
                                            aw_f[:, k], start=(k == 0), stop=(k == C - 1))
                last.then_inc(fold_done, 1)

            pe.wait_ge(consts, 6)
            pe.wait_ge(consts2, 7)

            def step(st):
                if st.has(-3):
                    if st.at(3):
                        pe.wait_ge(w_lo, 3)
                        pe.wait_ge(bk_split, 2)
                    pe.wait_ge(wsm_ready, st.done(-2) if st.has(-2) else st.done(-3))
                    pe.wait_ge(xn1_ready, st.done(-3))
                    transpose_h(T1h, xn1).then_inc(tr1_done, 1)
                if st.has(-1):
                    if st.has(-4):
                        pe.wait_ge(p2_hi_ready, st.done(-4))
                    pe.wait_ge(w_ready, st.done(-1))
                    nc.tensor.transpose(CC[:, 1, 0:N], wcol[:, :], ident[:, :]).then_inc(wt_done, 1)
                if st.has(0):
                    if st.at(0):
                        pe.wait_ge(w_lo, 1)
                    if st.has(-4):
                        pe.wait_ge(exps_ready, st.done(-4))
                    pe.wait_ge(h0_lo_ready, st.done(0))
                    weigh(A[:, 0, 0:QKV], 0, h0_hi, h0_lo, w0_hi, w0_lo)
                if st.has(-4):
                    pe.wait_ge(t_ready, st.done(-4))
                    for g in range(G):
                        last = nc.tensor.transpose(T0t[:, g], tnat[:, g], ident[:, :])
                    last.then_inc(tt_done, 1)
                if st.has(0):
                    weigh(A[:, 1, 0:QKV], 1, h0_hi, h0_lo, w0_hi, w0_lo).then_inc(qkv_done, 1)
                if st.has(-1):
                    if st.has(-3):
                        pe.wait_ge(h1_lo_ready, st.done(-3))
                    pe.wait_ge(wdiag_ready, st.done(-1))
                    nc.tensor.matmul(T1[:, 0:G], wexp[:, :], wdiag[:, :], start=True, stop=True).then_inc(wb_done, 1)
                if st.has(-4):
                    pe.wait_ge(p2_lo_ready, st.done(-4))
                    pe.wait_ge(tt_lo_ready, st.done(-4))
                    for g in range(G):
                        last = propagate(DD[:, g, D:2 * D], g, p2_hi, p2_lo)
                    last.then_inc(u_done, 1)
                if st.has(-3):
                    if st.has(-4):
                        pe.wait_ge(p2_hi_ready, st.done(-4))
                    pe.wait_ge(h1_lo_ready, st.done(-3))
                    for g in range(G):
                        last = weigh(CC[:, g, 0:PS], g, h1_hi, h1_lo, w2_hi, w2_lo)
                    last.then_inc(p2_done, 1)
                if st.has(0):
                    pe.wait_ge(adj_in[st.slot(0)], st.landed(0))
                    pe.wait_ge(qkv_saved, st.done(0))
                    for g in range(G):
                        last = nc.tensor.matmul(A[:, g, AK:AK + E], adjs[:, st.slot(0), g, 0:N],
                                                qkvs[:, st.j % 2, g, E:E2], start=True, stop=True)
                    last.then_inc(adjk_done, 1)
                if st.has(-4):
                    pe.wait_ge(u_lo_ready, st.done(-4))
                    for g in range(G):
                        propagate(DD[:, g, 0:D], g, u_hi, u_lo, skip_group_check=True).then_inc(h_done[g], 1)
                if st.has(1):
                    pe.wait_ge(xn0_ready, st.done(1))
                    transpose_h(T0h, xn0).then_inc(tr0_done, 1)
                if st.has(-3):
                    if st.has(0):
                        pe.wait_ge(w_ready, st.done(0))
                    pe.wait_ge(p2_saved, st.done(-3))
                    for g in range(G):
                        last = nc.tensor.transpose(A[:, g, 0:N], p2s[:, g, SJ:SJ + 1].broadcast_to([P, P]),
                                                   ident[:, :])
                    last.then_inc(sjt_done, 1)
                    for g in range(G):
                        if st.has(-4):
                            pe.wait_ge(y_ready[g], st.done(-4))
                        weigh(DD[:, g], g, h1_hi, h1_lo, w01_hi, w01_lo, stop=False)
                        nc.tensor.matmul(DD[:, g, 0:D], ones_r[:, :], bk_r[:, :], start=False, stop=False)
                if st.at(0):
                    fold_attention_weights()

            over_steps(pe, PAIRS, step)


def kernel(x, adj, L0_gnn_W_qk, L0_gnn_W_v, L1_gnn_Wv, L1_gnn_bv, L1_gnn_aw, L1_gnn_ab, L1_gnn_Wk, L1_gnn_bk):
    import concourse.bacc as bacc
    from concourse.bass_utils import run_bass_kernel_spmd

    nc = bacc.Bacc("TRN2", target_bir_lowering=False, num_devices=1)
    adj = np.asarray(adj)
    host = {
        "x": np.asarray(x),
        "adj2": np.stack([adj.transpose(0, 2, 1), adj], axis=2),
        "wqk_t": np.asarray(L0_gnn_W_qk).T,
        "wv_t": np.asarray(L0_gnn_W_v).T,
        "w1v_t": np.asarray(L1_gnn_Wv).T,
        "w1_bv": np.asarray(L1_gnn_bv).reshape(-1, P).T,
        "w1_aw": np.asarray(L1_gnn_aw).reshape(2, -1).T,
        "w1_ab": np.asarray(L1_gnn_ab),
        "w1_wk": np.asarray(L1_gnn_Wk),
        "w1_bk": np.asarray(L1_gnn_bk),
    }
    arrays, args = {}, []
    for name, a in host.items():
        arrays[f"{name}_dram"] = np.ascontiguousarray(a)
        args.append(nc.dram_tensor(f"{name}_dram", a.shape, mybir.dt.from_np(a.dtype), kind="ExternalInput").ap())
    args.append(nc.dram_tensor("out_dram", host["x"].shape, F32, kind="ExternalOutput").ap())
    build(nc, *args)
    result = run_bass_kernel_spmd(nc, [arrays], core_ids=[0])
    return result.results[0]["out_dram"]
```

```python
from collections import namedtuple
from contextlib import ExitStack

import numpy as np

import concourse.bass as bass
from concourse import mybir

ALU = mybir.AluOpType
ACT = mybir.ActivationFunctionType
AX_X = mybir.AxisListType.X
F32 = mybir.dt.float32
F32R = mybir.dt.float32r

P = 128
G = 2
RING = 4
EPS = 1e-5
SLOPE = 0.2
WARM_UP = 17
TINY = 1e-12


class Step(namedtuple("Step", "base j pairs peeled")):

    def has(self, off):
        return not self.peeled or 0 <= self.base + self.j + off < self.pairs

    def pair(self, off):
        return self.base + (self.j + off)

    def slot(self, off):
        return (self.j + off) % RING

    def done(self, off):
        return self.base + (self.j + off + 1)

    def stepped(self, back=0):
        return self.base + (self.j + 1 - FIRST - back)

    def landed(self, off):
        return self.base * (16 // RING) + 16 * ((self.j + off) // RING + 1)

    @property
    def filling(self):
        return self.peeled and self.base + self.j < RING - 1

    def at(self, number):
        return self.peeled and self.base + self.j == number


FIRST = -2


def over_steps(eng, pairs, step):
    last = pairs + 4
    lo, hi = 2 * RING, (pairs - 3) // RING * RING
    for s in range(FIRST, lo):
        step(Step(s // RING * RING, s % RING, pairs, True))
    with eng.Fori(lo // RING, hi // RING) as turn:
        for j in range(RING):
            step(Step(turn * RING, j, pairs, False))
    for s in range(hi, last):
        step(Step(s // RING * RING, s % RING, pairs, True))


def build(nc, x, adj2, wqk_t, wv_t, w1v_t, w1_bv, w1_aw, w1_ab, w1_wk, w1_bk, out):
    B, N, D = x.shape
    E2 = wqk_t.shape[1]
    E = E2 // 2
    K = w1_wk.shape[0]
    PAIRS = B // G
    C = D // P
    assert N == P and D == 2 * P and E2 == P and K == 3 and B % (G * RING) == 0
    QKV = E2 + D
    PS = D + 2
    SJ, SI = D, D + 1
    SCORE = 1.0 / float(E) ** 0.5

    x_pairs = x.rearrange("(p g) n d -> p n g d", g=G)
    out_pairs = out.rearrange("(p g) n d -> p n g d", g=G)
    adj_pairs = adj2.rearrange("(p g) n t m -> p n g (t m)", g=G)

    with ExitStack() as ctx:
        def sb(name, shape, dt=F32):
            return ctx.enter_context(nc.sbuf_tensor(name, shape, dt))

        def ps(name, shape):
            return ctx.enter_context(nc.psum_tensor(name, shape, F32))

        def sem(name):
            return ctx.enter_context(nc.semaphore(name))

        ident = sb("ident", [P, P])
        eps_c = sb("eps_c", [P, 2 * G])
        mhalf = sb("mhalf", [P, 2 * G])
        zero_c = sb("zero_c", [P, 2 * G])
        slope_c = sb("slope_c", [P, G])
        ones_k = sb("ones_k", [K, P])
        w0_f = sb("w0_f", [P, C, QKV])
        w2_f = sb("w2_f", [P, C, PS])
        w01_f = sb("w01_f", [P, C, 2 * D])
        w0_hi, w0_lo = sb("w0_hi", [P, C, QKV], F32R), sb("w0_lo", [P, C, QKV], F32R)
        w2_hi, w2_lo = sb("w2_hi", [P, C, PS], F32R), sb("w2_lo", [P, C, PS], F32R)
        w01_hi, w01_lo = sb("w01_hi", [P, C, 2 * D], F32R), sb("w01_lo", [P, C, 2 * D], F32R)
        wvt_f = sb("wvt_f", [P, C, D])
        aw_f = sb("aw_f", [P, C, 2])
        bv_f = sb("bv_f", [P, C])
        ab_f = sb("ab_f", [P, 1])
        bk_f = sb("bk_f", [K, D])
        bk_sum = sb("bk_sum", [P, D])
        e_const = sb("e_const", [P, 1])
        e_part, e_sum = sb("e_part", [P, 2]), sb("e_sum", [P, 1])

        xs = sb("xs", [P, RING, G, D])
        adjs = sb("adjs", [P, RING, G, 2 * N])
        x1s = sb("x1s", [P, RING, G, D])
        qkvs = sb("qkvs", [P, 2, G, QKV])

        stats = sb("stats", [P, 2, G, 6])
        carrier = sb("carrier", [P, 1])
        mv = sb("mv", [P, 2, G, 2])
        vareps, rstd = sb("vareps", [P, 2, G]), sb("rstd", [P, 2, G])
        mr, nmr = sb("mr", [P, 2, G]), sb("nmr", [P, 2, G])
        xn0, xn1 = sb("xn0", [P, G, D]), sb("xn1", [P, G, D])
        h0_hi, h0_lo = sb("h0_hi", [P, C, G, N], F32R), sb("h0_lo", [P, C, G, N], F32R)
        h1_hi, h1_lo = sb("h1_hi", [P, C, G, N], F32R), sb("h1_lo", [P, C, G, N], F32R)
        qak = sb("qak", [P, G, E])
        wcol = sb("wcol", [P, P])
        wmax, wbias = sb("wmax", [G, 1]), sb("wbias", [G, 1])
        wexp = sb("wexp", [G, N])
        wprob = sb("wprob", [P, N])
        wden, wrec = sb("wden", [G, 1]), sb("wrec", [G, 1])
        wsm = sb("wsm", [P, G])
        p2s = sb("p2s", [P, G, PS])
        p2_hi, p2_lo = sb("p2_hi", [P, G, D], F32R), sb("p2_lo", [P, G, D], F32R)
        b1, b2 = sb("b1", [P, G]), sb("b2", [P, G])
        e1, e2, emax = sb("e1", [P, G, N]), sb("e2", [P, G, N]), sb("emax", [P, G, N])
        alpha, tnat = sb("alpha", [P, G, N]), sb("tnat", [P, G, N])
        tt_hi, tt_lo = sb("tt_hi", [P, G, N], F32R), sb("tt_lo", [P, G, N], F32R)
        rsum, rsum1, rinv = sb("rsum", [P, G]), sb("rsum1", [P, G]), sb("rinv", [P, G])
        hb = sb("hb", [P, G, D])
        u_hi, u_lo = sb("u_hi", [P, G, D], F32R), sb("u_lo", [P, G, D], F32R)

        A = ps("A", [P, G, 512])
        AK = QKV
        CC = ps("CC", [P, G, 512])
        DD = ps("DD", [P, G, 512])
        T0 = ps("T0", [P, 512])
        T1 = ps("T1", [P, 512])
        T0h = T0[:, :].rearrange("p (c g n) -> p c g n", c=C, g=G)
        T1h = T1[:, :].rearrange("p (c g n) -> p c g n", c=C, g=G)
        T0t = T0[:, 0:G * N].rearrange("p (g n) -> p g n", g=G)

        x_in = [sem(f"x_in{r}") for r in range(RING)]
        adj_in = [sem(f"adj_in{r}") for r in range(RING)]
        out_done = [sem(f"out_done{r}") for r in range(RING)]
        w0_in, fold_in, w01_in, w2_in = sem("w0_in"), sem("fold_in"), sem("w01_in"), sem("w2_in")
        consts, consts2 = sem("consts"), sem("consts2")
        fold_done, e_const_ready, w_hi, w_lo = sem("fold_done"), sem("e_const_ready"), sem("w_hi"), sem("w_lo")
        w2_ready, bk_sum_ready = sem("w2_ready"), sem("bk_sum_ready")
        stats0_ready, stats1_ready, xn0_ready, xn1_ready = (
            sem("stats0_ready"), sem("stats1_ready"), sem("xn0_ready"), sem("xn1_ready"))
        mv_ready, vareps_ready, rstd_ready, mr_ready, norm_ready = (
            sem("mv_ready"), sem("vareps_ready"), sem("rstd_ready"), sem("mr_ready"), sem("norm_ready"))
        tr0_done, h0_hi_ready, h0_lo_ready = sem("tr0_done"), sem("h0_hi_ready"), sem("h0_lo_ready")
        tr1_done, h1_hi_ready, h1_lo_ready = sem("tr1_done"), sem("h1_hi_ready"), sem("h1_lo_ready")
        qkv_done, qkv_saved, adjk_done, w_ready = (sem("qkv_done"), sem("qkv_saved"), sem("adjk_done"),
                                                   sem("w_ready"))
        wt_done, wmax_ready, wbias_ready, wexp_ready = (sem("wt_done"), sem("wmax_ready"), sem("wbias_ready"),
                                                        sem("wexp_ready"))
        wrec_ready, wprob_ready, wb_done, wsm_ready, x1_ready = (
            sem("wrec_ready"), sem("wprob_ready"), sem("wb_done"), sem("wsm_ready"), sem("x1_ready"))
        p2_done, p2_saved, p2_hi_ready, p2_lo_ready = (sem("p2_done"), sem("p2_saved"), sem("p2_hi_ready"),
                                                       sem("p2_lo_ready"))
        sjt_done, b1_ready, bias_ready, exps_ready = (sem("sjt_done"), sem("b1_ready"), sem("bias_ready"),
                                                      sem("exps_ready"))
        emax_ready, alpha_ready, rsum1_ready, rinv_ready, t_ready = (
            sem("emax_ready"), sem("alpha_ready"), sem("rsum1_ready"), sem("rinv_ready"), sem("t_ready"))
        tt_done, tt_hi_ready, tt_lo_ready = sem("tt_done"), sem("tt_hi_ready"), sem("tt_lo_ready")
        u_done, u_hi_ready, u_lo_ready = sem("u_done"), sem("u_hi_ready"), sem("u_lo_ready")
        h_done = [sem(f"h_done{g}") for g in range(G)]
        hb_ready = [sem(f"hb_ready{g}") for g in range(G)]
        y_ready = sem("y_ready")

        block = ctx.enter_context(nc.Block())

        @block.sync
        def _(sp):
            def load_x(pair, slot):
                sp.dma_start(xs[:, slot], x_pairs[pair]).then_inc(x_in[slot], 16)

            def load_adj(pair, slot):
                sp.dma_start(adjs[:, slot], adj_pairs[pair]).then_inc(adj_in[slot], 16)

            load_x(0, 0)
            sp.dma_start(w0_f[:, :, 0:E2], wqk_t.rearrange("(c p) e -> p c e", p=P)).then_inc(w0_in, 16)
            sp.dma_start(w0_f[:, :, E2:QKV], wv_t.rearrange("(c p) e -> p c e", p=P)).then_inc(w0_in, 16)
            load_x(1, 1)
            sp.dma_start(wvt_f[:, :, :], w1v_t.rearrange("(c p) e -> p c e", p=P)).then_inc(fold_in, 16)
            sp.dma_start(aw_f[:, :, :], w1_aw.rearrange("(c p) t -> p c t", p=P)).then_inc(fold_in, 16)
            sp.dma_start(bv_f[:, :], w1_bv[:, :]).then_inc(fold_in, 16)
            sp.dma_start(ab_f[:, :], w1_ab.rearrange("(a o) -> a o", a=1).broadcast_to([P, 1])).then_inc(fold_in, 16)
            load_x(2, 2)
            wk_v = w1_wk.rearrange("k (c p) e -> k p c e", p=P)
            for k in range(2):
                sp.dma_start(w01_f[:, :, k * D:(k + 1) * D], wk_v[k]).then_inc(w01_in, 16)
            sp.dma_start(bk_f[:, :], w1_bk[:, :]).then_inc(fold_in, 16)
            sp.dma_start(w2_f[:, :, 0:D], wk_v[2]).then_inc(w2_in, 16)
            load_adj(0, 0)

            def step(st):
                if st.has(3) and st.has(0):
                    if st.has(-1):
                        sp.wait_ge(x1_ready, st.done(-1))
                    load_x(st.pair(3), st.slot(3))
                if st.has(1) and st.has(0):
                    if st.has(-3):
                        sp.wait_ge(alpha_ready, st.done(-3))
                    load_adj(st.pair(1), st.slot(1))
                if st.has(-4):
                    sp.wait_ge(y_ready, st.done(-4))
                    sp.dma_start(out_pairs[st.pair(-4)], x1s[:, st.slot(-4)]).then_inc(out_done[st.slot(-4)], 16)

            over_steps(sp, PAIRS, step)
            for r in range(RING):
                sp.wait_ge(out_done[r], 16 * (PAIRS // RING))

        @block.gpsimd
        def _(pool):
            pool.memset(ident[:, :], 0.0).then_inc(consts, 1)
            pool.wait_ge(consts, 1)
            pool.affine_select(out=ident[:, :], in_=ident[:, :], compare_op=ALU.not_equal, fill=1.0, base=0,
                               pattern=[[-1, P]], channel_multiplier=1).then_inc(consts, 1)
            pool.memset(eps_c[:, :], EPS).then_inc(consts, 1)
            pool.memset(mhalf[:, :], -0.5).then_inc(consts, 1)
            pool.memset(zero_c[:, :], 0.0).then_inc(consts, 1)
            pool.memset(slope_c[:, :], SLOPE).then_inc(consts, 1)
            pool.wait_ge(consts, 6)

            def step(st):
                if st.at(1):
                    pool.wait_ge(w_hi, 2)
                    pool.tensor_tensor(out=w01_lo[:, :, :], in0=w01_f[:, :, :], in1=w01_hi[:, :, :].bitcast(F32),
                                       op=ALU.subtract).then_inc(w_lo, 1)
                    pool.wait_ge(w_hi, 3)
                    pool.tensor_tensor(out=w2_lo[:, :, :], in0=w2_f[:, :, :], in1=w2_hi[:, :, :].bitcast(F32),
                                       op=ALU.subtract).then_inc(w_lo, 1)
                if st.has(2) or st.has(-2):
                    pool.wait_ge(mv_ready, st.stepped())
                    pool.tensor_tensor(out=vareps[:, :, :].rearrange("p l g -> p (l g)"),
                                       in0=mv[:, :, :, 1].rearrange("p l g -> p (l g)"),
                                       in1=eps_c[:, :], op=ALU.add).then_inc(vareps_ready, 1)
                if st.has(-3):
                    if st.at(3):
                        pool.wait_ge(e_const_ready, 3)
                    pool.wait_ge(p2_saved, st.done(-3))
                    pool.tensor_tensor(out=b1[:, :], in0=p2s[:, :, SI], in1=e_const[:, :].broadcast_to([P, G]),
                                       op=ALU.add).then_inc(b1_ready, 1)
                    pool.wait_ge(b1_ready, st.done(-3))
                    pool.tensor_tensor(out=b2[:, :], in0=b1[:, :], in1=slope_c[:, :],
                                       op=ALU.mult).then_inc(bias_ready, 1)
                if st.has(2) or st.has(-2):
                    if st.has(1):
                        pool.wait_ge(xn0_ready, st.done(1))
                    if st.has(-3):
                        pool.wait_ge(xn1_ready, st.done(-3))
                    pool.wait_ge(vareps_ready, st.stepped())
                    pool.tensor_tensor(out=rstd[:, :, :].rearrange("p l g -> p (l g)"),
                                       in0=vareps[:, :, :].rearrange("p l g -> p (l g)"),
                                       in1=mhalf[:, :], op=ALU.pow).then_inc(rstd_ready, 1)
                    pool.wait_ge(rstd_ready, st.stepped())
                    pool.tensor_tensor(out=mr[:, :, :].rearrange("p l g -> p (l g)"),
                                       in0=mv[:, :, :, 0].rearrange("p l g -> p (l g)"),
                                       in1=rstd[:, :, :].rearrange("p l g -> p (l g)"),
                                       op=ALU.mult).then_inc(mr_ready, 1)
                    pool.wait_ge(mr_ready, st.stepped())
                    pool.tensor_tensor(out=nmr[:, :, :].rearrange("p l g -> p (l g)"), in0=zero_c[:, :],
                                       in1=mr[:, :, :].rearrange("p l g -> p (l g)"),
                                       op=ALU.subtract).then_inc(norm_ready, 1)
                if st.has(-3):
                    pool.wait_ge(p2_hi_ready, st.done(-3))
                    pool.tensor_tensor(out=p2_lo[:, :, :], in0=p2s[:, :, 0:D], in1=p2_hi[:, :, :].bitcast(F32),
                                       op=ALU.subtract).then_inc(p2_lo_ready, 1)

            over_steps(pool, PAIRS, step)

        @block.scalar
        def _(act):
            def norm_x(st):
                act.wait_ge(norm_ready, st.stepped(1))
                for g in range(G):
                    last = act.activation(xn0[:, g], xs[:, st.slot(1), g], ACT.Identity,
                                          bias=nmr[:, 0, g:g + 1], scale=rstd[:, 0, g:g + 1])
                last.then_inc(xn0_ready, 1)

            def step(st):
                if st.at(FIRST):
                    act.wait_ge(w0_in, 32)
                    act.activation(w0_hi[:, :, :], w0_f[:, :, :], ACT.Copy).then_inc(w_hi, 1)
                if st.at(0):
                    act.wait_ge(w01_in, 32)
                    act.activation(w01_hi[:, :, :], w01_f[:, :, :], ACT.Copy).then_inc(w_hi, 1)
                if st.at(1):
                    act.wait_ge(w2_ready, 1)
                    act.activation(w2_hi[:, :, :], w2_f[:, :, :], ACT.Copy).then_inc(w_hi, 1)
                if st.has(-4):
                    act.wait_ge(rinv_ready, st.done(-4))
                    for g in range(G):
                        last = act.activation(tnat[:, g], alpha[:, g], ACT.Copy, scale=rinv[:, g:g + 1])
                    last.then_inc(t_ready, 1)
                if st.has(-3):
                    act.wait_ge(tr1_done, st.done(-3))
                    act.activation(h1_hi[:, :, :, :], T1h, ACT.Relu).then_inc(h1_hi_ready, 1)
                if st.has(-4):
                    act.wait_ge(tt_done, st.done(-4))
                    act.activation(tt_hi[:, :, :], T0t, ACT.Copy).then_inc(tt_hi_ready, 1)
                if st.has(-1):
                    act.wait_ge(wbias_ready, st.done(-1))
                    act.activation(wexp[:, :], CC[0:G, 1, 0:N], ACT.Exp, bias=wbias[:, :], scale=SCORE,
                                   accum_out=wden[:, :]).then_inc(wexp_ready, 1)
                if st.has(1) and st.filling:
                    norm_x(st)
                if st.has(0):
                    act.wait_ge(qkv_done, st.done(0))
                    act.activation(qkvs[:, st.j % 2], A[:, :, 0:QKV], ACT.Copy).then_inc(qkv_saved, 1)
                if st.has(-4):
                    act.wait_ge(u_done, st.done(-4))
                    act.activation(u_hi[:, :, :], DD[:, :, D:2 * D], ACT.Copy).then_inc(u_hi_ready, 1)
                if st.has(1) and not st.filling:
                    norm_x(st)
                if st.has(-3):
                    act.wait_ge(p2_done, st.done(-3))
                    if st.has(-4):
                        act.wait_ge(p2_lo_ready, st.done(-4))
                    act.activation(p2s[:, :, :], CC[:, :, 0:PS], ACT.Copy).then_inc(p2_saved, 1)
                    act.activation(p2_hi[:, :, :], CC[:, :, 0:D], ACT.Copy).then_inc(p2_hi_ready, 1)
                if st.has(-3):
                    act.wait_ge(bias_ready, st.done(-3))
                    act.wait_ge(sjt_done, st.done(-3))
                    for g in range(G):
                        act.activation(e1[:, g], A[:, g, 0:N], ACT.Exp, bias=b1[:, g:g + 1])
                        last = act.activation(e2[:, g], A[:, g, 0:N], ACT.Exp, bias=b2[:, g:g + 1], scale=SLOPE)
                    last.then_inc(exps_ready, 1)
                if st.has(1):
                    act.wait_ge(tr0_done, st.done(1))
                    act.activation(h0_hi[:, :, :, :], T0h, ACT.Relu).then_inc(h0_hi_ready, 1)
                if st.has(-2):
                    act.wait_ge(norm_ready, st.stepped())
                    for g in range(G):
                        last = act.activation(xn1[:, g], x1s[:, st.slot(-2), g], ACT.Identity,
                                              bias=nmr[:, 1, g:g + 1], scale=rstd[:, 1, g:g + 1])
                    last.then_inc(xn1_ready, 1)

            over_steps(act, PAIRS, step)

        @block.vector
        def _(dve):
            dve.memset(ones_k[:, :], 1.0).then_inc(consts2, 1)
            dve.memset(wcol[:, :], 0.0).then_inc(consts2, 1)
            dve.memset(mv[:, :, :, :], 1.0).then_inc(consts2, 1)
            dve.memset(wprob[:, :], 0.0).then_inc(consts2, 1)
            dve.wait_ge(consts2, 4)

            def read_softmax(st):
                dve.wait_ge(wb_done, st.done(-1))
                dve.tensor_copy(out=wsm[:, :], in_=T1[:, 0:G]).then_inc(wsm_ready, 1)

            def make_x1(st):
                if st.has(-5):
                    dve.wait_ge(out_done[st.slot(-5)], st.landed(-5))
                dve.wait_ge(wsm_ready, st.done(-1))
                for g in range(G):
                    last = dve.scalar_tensor_tensor(out=x1s[:, st.slot(-1), g],
                                                    in0=qkvs[:, (st.j - 1) % 2, g, E2:QKV],
                                                    scalar=wsm[:, g:g + 1], in1=xs[:, st.slot(-1), g],
                                                    op0=ALU.mult, op1=ALU.add)
                last.then_inc(x1_ready, 1)

            def split_w0():
                dve.wait_ge(w_hi, 1)
                dve.tensor_tensor(out=w0_lo[:, :, :], in0=w0_f[:, :, :], in1=w0_hi[:, :, :].bitcast(F32),
                                  op=ALU.subtract).then_inc(w_lo, 1)

            def fold_attention_constants():
                dve.wait_ge(w2_in, 16)
                dve.wait_ge(fold_done, 1)
                dve.tensor_copy(out=w2_f[:, :, D:PS], in_=DD[:, 0, 0:2 * C].rearrange("p (c t) -> p c t", c=C)
                                ).then_inc(w2_ready, 1)
                dve.tensor_copy(out=bk_sum[:, :], in_=DD[:, 0, D:2 * D]).then_inc(bk_sum_ready, 1)
                dve.tensor_copy(out=e_part[:, :], in_=DD[:, 0, 2 * C:2 * C + 2]).then_inc(e_const_ready, 1)
                dve.wait_ge(e_const_ready, 1)
                dve.tensor_tensor(out=e_sum[:, :], in0=e_part[:, 0:1], in1=e_part[:, 1:2],
                                  op=ALU.add).then_inc(e_const_ready, 1)
                dve.wait_ge(e_const_ready, 2)
                dve.tensor_tensor(out=e_const[:, :], in0=e_sum[:, :], in1=ab_f[:, :],
                                  op=ALU.add).then_inc(e_const_ready, 1)

            def step(st):
                if st.has(-3):
                    dve.wait_ge(h1_hi_ready, st.done(-3))
                    dve.scalar_tensor_tensor(out=h1_lo[:, :, :, :].rearrange("p c g n -> p (c g n)"), in0=T1[:, :],
                                             scalar=0.0,
                                             in1=h1_hi[:, :, :, :].rearrange("p c g n -> p (c g n)").bitcast(F32),
                                             op0=ALU.max, op1=ALU.subtract).then_inc(h1_lo_ready, 1)
                if st.has(-4):
                    dve.wait_ge(tt_hi_ready, st.done(-4))
                    dve.tensor_tensor(out=tt_lo[:, :, :], in0=T0t, in1=tt_hi[:, :, :].bitcast(F32),
                                      op=ALU.subtract).then_inc(tt_lo_ready, 1)
                if st.has(-2):
                    dve.wait_ge(x1_ready, st.done(-2))
                    dve.wait_ge(mv_ready, st.stepped(1))
                    for g in range(G):
                        last = dve.bn_stats(out=stats[:, 1, g], in_=x1s[:, st.slot(-2), g])
                    last.then_inc(stats1_ready, 1)
                if st.has(-1):
                    dve.wait_ge(wexp_ready, st.done(-1))
                    dve.reciprocal(out=wrec[:, :], in_=wden[:, :]).then_inc(wrec_ready, 1)
                    dve.wait_ge(wrec_ready, st.done(-1))
                    dve.tensor_scalar(out=wprob[0:G, :], in0=wexp[:, :], scalar1=wrec[:, :], scalar2=None,
                                      op0=ALU.mult).then_inc(wprob_ready, 1)
                if st.has(2):
                    if st.has(1):
                        dve.wait_ge(mv_ready, st.stepped(1))
                    dve.wait_ge(x_in[st.slot(2)], st.landed(2))
                    for g in range(G):
                        last = dve.bn_stats(out=stats[:, 0, g], in_=xs[:, st.slot(2), g])
                    last.then_inc(stats0_ready, 1)
                if st.has(-4):
                    dve.wait_ge(u_hi_ready, st.done(-4))
                    dve.tensor_tensor(out=u_lo[:, :, :], in0=DD[:, :, D:2 * D], in1=u_hi[:, :, :].bitcast(F32),
                                      op=ALU.subtract).then_inc(u_lo_ready, 1)
                if st.has(2) or st.has(-2):
                    if not st.at(FIRST):
                        dve.wait_ge(norm_ready, st.stepped(1))
                    if st.has(2):
                        dve.wait_ge(stats0_ready, st.done(2))
                    else:
                        dve.wait_ge(stats1_ready, st.done(-2))
                    dve.memset(carrier[:, :], 0.0)
                    for layer in ([0] if st.has(2) else []) + ([1] if st.has(-2) else []):
                        for g in range(G):
                            last = dve.bn_aggr(out=mv[:, layer, g], in_=stats[:, layer, g])
                    last.then_inc(mv_ready, 1)
                if st.at(FIRST):
                    split_w0()
                if st.has(-1) and st.filling:
                    read_softmax(st)
                    make_x1(st)
                if st.has(0):
                    dve.wait_ge(adjk_done, st.done(0))
                    for g in range(G):
                        last = dve.scalar_tensor_tensor(out=qak[:, g], in0=A[:, g, AK:AK + E], scalar=1.0,
                                                        in1=qkvs[:, st.j % 2, g, 0:E], op0=ALU.mult, op1=ALU.mult,
                                                        accum_out=wcol[:, g:g + 1])
                    last.then_inc(w_ready, 1)

                def add_bias(g):
                    dve.wait_ge(h_done[g], st.done(-4))
                    dve.tensor_tensor(out=hb[:, g], in0=DD[:, g, 0:D], in1=bk_sum[:, :],
                                      op=ALU.add).then_inc(hb_ready[g], 1)

                if st.has(-1) and not st.filling:
                    read_softmax(st)
                if st.has(-4):
                    if st.at(4):
                        dve.wait_ge(bk_sum_ready, 1)
                    else:
                        dve.wait_ge(y_ready, st.done(-5))
                    add_bias(0)
                if st.has(-1) and not st.filling:
                    make_x1(st)
                if st.has(-4):
                    add_bias(1)
                if st.has(-3):
                    dve.wait_ge(exps_ready, st.done(-3))
                    dve.tensor_tensor(out=emax[:, :, :], in0=e1[:, :, :], in1=e2[:, :, :],
                                      op=ALU.max).then_inc(emax_ready, 1)
                    if st.has(-4):
                        dve.wait_ge(t_ready, st.done(-4))
                    dve.wait_ge(adj_in[st.slot(-3)], st.landed(-3))
                    dve.wait_ge(emax_ready, st.done(-3))
                    for g in range(G):
                        last = dve.scalar_tensor_tensor(out=alpha[:, g], in0=emax[:, g], scalar=1.0,
                                                        in1=adjs[:, st.slot(-3), g, N:2 * N], op0=ALU.mult,
                                                        op1=ALU.mult, accum_out=rsum[:, g:g + 1])
                    last.then_inc(alpha_ready, 1)
                    dve.wait_ge(alpha_ready, st.done(-3))
                    dve.tensor_scalar(out=rsum1[:, :], in0=rsum[:, :], scalar1=TINY, scalar2=None,
                                      op0=ALU.add).then_inc(rsum1_ready, 1)
                    dve.wait_ge(rsum1_ready, st.done(-3))
                    dve.reciprocal(out=rinv[:, :], in_=rsum1[:, :]).then_inc(rinv_ready, 1)
                if st.has(0):
                    dve.wait_ge(wt_done, st.done(0))
                    dve.reduce_max(wmax[:, :], CC[0:G, 1, 0:N], AX_X).then_inc(wmax_ready, 1)
                if st.has(1):
                    dve.wait_ge(h0_hi_ready, st.done(1))
                    dve.scalar_tensor_tensor(out=h0_lo[:, :, :, :].rearrange("p c g n -> p (c g n)"), in0=T0[:, :],
                                             scalar=0.0,
                                             in1=h0_hi[:, :, :, :].rearrange("p c g n -> p (c g n)").bitcast(F32),
                                             op0=ALU.max, op1=ALU.subtract).then_inc(h0_lo_ready, 1)
                if st.has(-4):
                    dve.wait_ge(hb_ready[G - 1], st.done(-4))
                    dve.scalar_tensor_tensor(out=x1s[:, st.slot(-4)], in0=hb[:, :, :], scalar=0.0,
                                             in1=x1s[:, st.slot(-4)], op0=ALU.max, op1=ALU.add).then_inc(y_ready, 1)
                if st.has(0):
                    dve.wait_ge(wmax_ready, st.done(0))
                    dve.tensor_scalar(out=wbias[:, :], in0=wmax[:, :], scalar1=-SCORE, scalar2=None,
                                      op0=ALU.mult).then_inc(wbias_ready, 1)
                if st.at(-1):
                    fold_attention_constants()

            over_steps(dve, PAIRS, step)

        @block.tensor
        def _(pe):
            def weigh_hi(out_, g, h_hi, w_hi_, w_lo_):
                for c in range(C):
                    for n, w in enumerate((w_hi_, w_lo_)):
                        nc.tensor.matmul(out_, h_hi[:, c, g], w[:, c], start=(c == 0 and n == 0), stop=False)

            def weigh_lo(out_, g, h_lo, w_hi_, stop=True):
                for c in range(C):
                    last = nc.tensor.matmul(out_, h_lo[:, c, g], w_hi_[:, c], start=False, stop=stop and c == C - 1)
                return last

            def propagate(out_, g, t, v, stop=False, **group):
                return nc.tensor.matmul(out_, t[:, g], v[:, g], start=False, stop=stop, **group)

            def transpose_h(out_, src):
                for c in range(C):
                    for g in range(G):
                        last = nc.tensor.transpose(out_[:, c, g], src[:, g, c * P:(c + 1) * P], ident[:, :])
                return last

            def softmax_to_columns(st):
                if st.has(-3):
                    pe.wait_ge(h1_lo_ready, st.done(-3))
                pe.wait_ge(wprob_ready, st.done(-1))
                nc.tensor.transpose(T1[:, 0:N], wprob[:, :], ident[:, :]).then_inc(wb_done, 1)

            def transpose_xn0(st):
                pe.wait_ge(xn0_ready, st.done(1))
                transpose_h(T0h, xn0).then_inc(tr0_done, 1)

            def qkv_hi(st):
                if st.at(0):
                    pe.wait_ge(w_lo, 1)
                if st.has(-4):
                    pe.wait_ge(exps_ready, st.done(-4))
                elif st.has(-1):
                    pe.wait_ge(w_ready, st.done(-1))
                pe.wait_ge(h0_hi_ready, st.done(0))
                weigh_hi(A[:, 0, 0:QKV], 0, h0_hi, w0_hi, w0_lo)

            def fold_attention_weights():
                pe.wait_ge(fold_in, 80)
                for c in range(C):
                    for k in range(C):
                        nc.tensor.matmul(DD[:, 0, 2 * c:2 * c + 2], wvt_f[:, k, c * P:(c + 1) * P], aw_f[:, k],
                                         start=(k == 0), stop=(k == C - 1))
                for k in range(C):
                    nc.tensor.matmul(DD[:, 0, 2 * C:2 * C + 2], bv_f[:, k:k + 1].broadcast_to([P, P]),
                                     aw_f[:, k], start=(k == 0), stop=(k == C - 1))
                nc.tensor.matmul(DD[:, 0, D:2 * D], ones_k[:, :], bk_f[:, :], start=True,
                                 stop=True).then_inc(fold_done, 1)

            pe.wait_ge(consts, 6)
            pe.wait_ge(consts2, 4)
            for _ in range(WARM_UP):
                nc.tensor.matmul(DD[:, 1, 0:P], ident[:, :], ident[:, :], start=True, stop=True)

            def step(st):
                if st.has(0) and (st.filling or st.at(3)):
                    qkv_hi(st)
                if st.has(-3):
                    if st.at(3):
                        pe.wait_ge(w_lo, 3)
                    pe.wait_ge(wsm_ready, st.done(-2) if st.has(-2) else st.done(-3))
                    pe.wait_ge(xn1_ready, st.done(-3))
                    transpose_h(T1h, xn1).then_inc(tr1_done, 1)
                if st.has(0) and not (st.filling or st.at(3)):
                    qkv_hi(st)
                if st.has(-4):
                    if st.has(0):
                        pe.wait_ge(h0_lo_ready, st.done(0))
                    pe.wait_ge(t_ready, st.done(-4))
                    for g in range(G):
                        last = nc.tensor.transpose(T0t[:, g], tnat[:, g], ident[:, :])
                    last.then_inc(tt_done, 1)
                if st.has(0):
                    pe.wait_ge(h0_lo_ready, st.done(0))
                    weigh_lo(A[:, 0, 0:QKV], 0, h0_lo, w0_hi)
                if st.has(0):
                    weigh_hi(A[:, 1, 0:QKV], 1, h0_hi, w0_hi, w0_lo)
                    weigh_lo(A[:, 1, 0:QKV], 1, h0_lo, w0_hi).then_inc(qkv_done, 1)
                if st.has(-4):
                    pe.wait_ge(p2_lo_ready, st.done(-4))
                    pe.wait_ge(tt_hi_ready, st.done(-4))
                    for g in range(G):
                        propagate(DD[:, g, D:2 * D], g, tt_hi, p2_hi)
                        propagate(DD[:, g, D:2 * D], g, tt_hi, p2_lo)
                    pe.wait_ge(tt_lo_ready, st.done(-4))
                    for g in range(G):
                        last = propagate(DD[:, g, D:2 * D], g, tt_lo, p2_hi, stop=True)
                    last.then_inc(u_done, 1)
                if st.has(-1) and st.filling:
                    softmax_to_columns(st)
                if st.has(-3):
                    if st.has(-1):
                        pe.wait_ge(wexp_ready, st.done(-1))
                    if st.has(-4):
                        pe.wait_ge(p2_hi_ready, st.done(-4))
                    pe.wait_ge(h1_lo_ready, st.done(-3))
                    for g in range(G):
                        weigh_hi(CC[:, g, 0:PS], g, h1_hi, w2_hi, w2_lo)
                        last = weigh_lo(CC[:, g, 0:PS], g, h1_lo, w2_hi)
                    last.then_inc(p2_done, 1)
                if st.has(1) and st.filling:
                    transpose_xn0(st)
                if st.has(0):
                    pe.wait_ge(adj_in[st.slot(0)], st.landed(0))
                    pe.wait_ge(qkv_saved, st.done(0))
                    for g in range(G):
                        last = nc.tensor.matmul(A[:, g, AK:AK + E], adjs[:, st.slot(0), g, 0:N],
                                                qkvs[:, st.j % 2, g, E:E2], start=True, stop=True)
                    last.then_inc(adjk_done, 1)
                if st.has(-1) and not st.filling:
                    softmax_to_columns(st)
                if st.has(-4):
                    pe.wait_ge(u_lo_ready, st.done(-4))
                    for g in range(G):
                        propagate(DD[:, g, 0:D], g, tt_hi, u_hi, skip_group_check=True)
                        propagate(DD[:, g, 0:D], g, tt_lo, u_hi, skip_group_check=True)
                        propagate(DD[:, g, 0:D], g, tt_hi, u_lo, stop=True,
                                  skip_group_check=True).then_inc(h_done[g], 1)
                if st.has(-3):
                    if st.has(0):
                        pe.wait_ge(w_ready, st.done(0))
                    pe.wait_ge(p2_saved, st.done(-3))
                    for g in range(G):
                        last = nc.tensor.transpose(A[:, g, 0:N], p2s[:, g, SJ:SJ + 1].broadcast_to([P, P]),
                                                   ident[:, :])
                    last.then_inc(sjt_done, 1)
                if st.has(1) and not st.filling:
                    transpose_xn0(st)
                if st.has(0):
                    if st.has(-3):
                        pe.wait_ge(p2_hi_ready, st.done(-3))
                    pe.wait_ge(w_ready, st.done(0))
                    nc.tensor.transpose(CC[:, 1, 0:N], wcol[:, :], ident[:, :]).then_inc(wt_done, 1)
                if st.has(-3):
                    for g in range(G):
                        if st.has(-4):
                            pe.wait_ge(hb_ready[g], st.done(-4))
                        weigh_hi(DD[:, g], g, h1_hi, w01_hi, w01_lo)
                        weigh_lo(DD[:, g], g, h1_lo, w01_hi, stop=False)
                if st.at(-1):
                    fold_attention_weights()

            over_steps(pe, PAIRS, step)


def kernel(x, adj, L0_gnn_W_qk, L0_gnn_W_v, L1_gnn_Wv, L1_gnn_bv, L1_gnn_aw, L1_gnn_ab, L1_gnn_Wk, L1_gnn_bk):
    import concourse.bacc as bacc
    from concourse.bass_utils import run_bass_kernel_spmd

    nc = bacc.Bacc("TRN2", target_bir_lowering=False, num_devices=1)
    adj = np.asarray(adj)
    host = {
        "x": np.asarray(x),
        "adj2": np.stack([adj.transpose(0, 2, 1), adj], axis=2),
        "wqk_t": np.asarray(L0_gnn_W_qk).T,
        "wv_t": np.asarray(L0_gnn_W_v).T,
        "w1v_t": np.asarray(L1_gnn_Wv).T,
        "w1_bv": np.asarray(L1_gnn_bv).reshape(-1, P).T,
        "w1_aw": np.asarray(L1_gnn_aw).reshape(2, -1).T,
        "w1_ab": np.asarray(L1_gnn_ab),
        "w1_wk": np.asarray(L1_gnn_Wk),
        "w1_bk": np.asarray(L1_gnn_bk),
    }
    arrays, args = {}, []
    for name, a in host.items():
        arrays[f"{name}_dram"] = np.ascontiguousarray(a)
        args.append(nc.dram_tensor(f"{name}_dram", a.shape, mybir.dt.from_np(a.dtype), kind="ExternalInput").ap())
    args.append(nc.dram_tensor("out_dram", host["x"].shape, F32, kind="ExternalOutput").ap())
    build(nc, *args)
    result = run_bass_kernel_spmd(nc, [arrays], core_ids=[0])
    return result.results[0]["out_dram"]
```
